# Optimizing a Trainium2 kernel written in Bass

```python
import numpy as np
import jax
import jax.numpy as jnp

def _softmax(x, axis=-1):
    return jax.nn.softmax(x, axis=axis)

def _gelu(x):
    return jax.nn.gelu(x, approximate=True)

def _silu(x):
    return jax.nn.silu(x)

def _sigmoid(x):
    return jax.nn.sigmoid(x)

def _layernorm(x, axis=-1, eps=1e-05):
    m = jnp.mean(x, axis=axis, keepdims=True)
    v = jnp.var(x, axis=axis, keepdims=True)
    return (x - m) / jnp.sqrt(v + eps)

def _scatter_add(tgt, idx, src, axis=0):
    return tgt.at[idx].add(src)

def _segment_sum(src, seg, n):
    return jax.ops.segment_sum(src, seg, n)
kernel_name = 'mk_gnn_resnorm_d1_gnn_r8_60a69c'

def setup_inputs(seed: int=0):
    np.random.seed(seed)
    _w = jnp.asarray

    def _rec_inputs():
        import jax
        import jax.numpy as jnp
        _gk = jax.random.key(seed)
        x = -0.000202 + 1 * jax.random.normal(jax.random.fold_in(_gk, 1), (6250, 128), jnp.float32)
        _s = jax.random.randint(jax.random.fold_in(_gk, 2), (100000,), 0, 6250, jnp.int32)
        _d = jax.random.randint(jax.random.fold_in(_gk, 3), (100000,), 0, 6250, jnp.int32)
        _loop = jnp.arange(6250, dtype=jnp.int32)
        src = jnp.concatenate([_s, _d, _loop])
        dst = jnp.concatenate([_d, _s, _loop])
        _o = jnp.argsort(dst, stable=True)
        src = src[_o]
        dst = dst[_o]
        edge_attr_128 = -8.16379e-05 + 0.999858 * jax.random.normal(jax.random.fold_in(_gk, 12), (206250, 128), jnp.float32)
        return (x, src, dst, edge_attr_128)
    x, src, dst, edge_attr_128 = _rec_inputs()

    def _L0_gnn_setup():
        import jax, jax.numpy as jnp
        import numpy as np
        N_NODES = 6250
        N_EDGES = 100000
        D_FEAT = 128
        N_HEADS = 4
        HEAD_DIM = 32

        def mish(x):
            return x * jnp.tanh(jax.nn.softplus(x))
        key = jax.random.key(seed)
        ks = jax.random.split(key, 12)
        s = 1.0 / np.sqrt(D_FEAT)
        return {'nodes': jax.random.normal(ks[0], (N_NODES, D_FEAT), jnp.float32), 'edges': jax.random.normal(ks[1], (N_EDGES, D_FEAT), jnp.float32), 'Ws_k': jax.random.normal(ks[2], (D_FEAT, N_HEADS, HEAD_DIM), jnp.float32) * s, 'Ws_b': jnp.zeros((N_HEADS, HEAD_DIM), jnp.float32), 'Wr_k': jax.random.normal(ks[3], (D_FEAT, N_HEADS, HEAD_DIM), jnp.float32) * s, 'Wr_b': jnp.zeros((N_HEADS, HEAD_DIM), jnp.float32), 'We_k': jax.random.normal(ks[4], (D_FEAT, N_HEADS, HEAD_DIM), jnp.float32) * s, 'We_b': jnp.zeros((N_HEADS, HEAD_DIM), jnp.float32), 'attn_w': jax.random.normal(ks[5], (HEAD_DIM, 1), jnp.float32) / np.sqrt(HEAD_DIM), 'attn_b': jnp.zeros((1,), jnp.float32), 'senders': jax.random.randint(ks[6], (N_EDGES,), 0, N_NODES, jnp.int32), 'receivers': jax.random.randint(ks[7], (N_EDGES,), 0, N_NODES, jnp.int32)}
    _L0_gnn_all = _L0_gnn_setup()
    _L0_gnn_in = {k: v for k, v in _L0_gnn_all.items() if k in ('Ws_k', 'Ws_b', 'Wr_k', 'Wr_b', 'We_k', 'We_b', 'attn_w', 'attn_b')}
    del _L0_gnn_all
    return {'x': x, 'src': src, 'dst': dst, 'edge_attr_128': edge_attr_128, 'L0_gnn_Ws_k': _L0_gnn_in['Ws_k'], 'L0_gnn_Ws_b': _L0_gnn_in['Ws_b'], 'L0_gnn_Wr_k': _L0_gnn_in['Wr_k'], 'L0_gnn_Wr_b': _L0_gnn_in['Wr_b'], 'L0_gnn_We_k': _L0_gnn_in['We_k'], 'L0_gnn_We_b': _L0_gnn_in['We_b'], 'L0_gnn_attn_w': _L0_gnn_in['attn_w'], 'L0_gnn_attn_b': _L0_gnn_in['attn_b']}

def reference(x, src, dst, edge_attr_128, L0_gnn_Ws_k, L0_gnn_Ws_b, L0_gnn_Wr_k, L0_gnn_Wr_b, L0_gnn_We_k, L0_gnn_We_b, L0_gnn_attn_w, L0_gnn_attn_b):
    import jax
    import jax.numpy as jnp

    def _L0_gnn_ref(nodes, edges, Ws_k, Ws_b, Wr_k, Wr_b, We_k, We_b, attn_w, attn_b, senders, receivers):
        import jax, jax.numpy as jnp
        import numpy as np
        N_NODES = 6250
        N_EDGES = 100000
        D_FEAT = 128
        N_HEADS = 4
        HEAD_DIM = 32

        def mish(x):
            return x * jnp.tanh(jax.nn.softplus(x))
        n = nodes.shape[0]
        sent = jnp.einsum('ef,fhd->ehd', nodes[senders], Ws_k) + Ws_b
        e_att = sent + jnp.einsum('ef,fhd->ehd', edges, We_k) + We_b
        recv = jnp.einsum('ef,fhd->ehd', nodes[receivers], Wr_k) + Wr_b
        logits = jnp.einsum('ehd,do->eho', mish(e_att + recv), attn_w) + attn_b
        seg_max = jax.ops.segment_max(logits, receivers, num_segments=n)
        w = jnp.exp(logits - seg_max[receivers])
        denom = jax.ops.segment_sum(w, receivers, num_segments=n)
        w = w / denom[receivers]
        msg = (w * e_att).reshape(e_att.shape[0], N_HEADS * HEAD_DIM)
        out_nodes = jax.ops.segment_sum(msg, receivers, num_segments=n)
        return out_nodes
    x = _layernorm(x + _L0_gnn_ref(x, edge_attr_128, L0_gnn_Ws_k, L0_gnn_Ws_b, L0_gnn_Wr_k, L0_gnn_Wr_b, L0_gnn_We_k, L0_gnn_We_b, L0_gnn_attn_w, L0_gnn_attn_b, src, dst), axis=-1)
    return x

_drawn_inputs = setup_inputs


def setup_inputs(seed=0):
    import zlib

    import numpy as np

    out = dict(_drawn_inputs(seed))
    spreads = {'L0_gnn_Ws_b': (0.0, 0.1), 'L0_gnn_Wr_b': (0.0, 0.539), 'L0_gnn_We_b': (0.0, 0.1)}
    factors = {}
    for name, (base, spread) in spreads.items():
        noise = np.random.default_rng([zlib.crc32(name.encode()), seed]).standard_normal(out[name].shape)
        drawn = base * np.exp(spread * noise) if base else spread * noise
        out[name] = jnp.asarray(drawn.astype(out[name].dtype))
    for name, factor in factors.items():
        out[name] = (out[name] * factor).astype(out[name].dtype)
    return out
```

```python
from contextlib import ExitStack

import concourse.bass as bass
from concourse import mybir

F32 = mybir.dt.float32
I32 = mybir.dt.int32
BF16 = mybir.dt.bfloat16
ALU = mybir.AluOpType
ACT = mybir.ActivationFunctionType
AX = mybir.AxisListType

P = 128
D = 128
H = 4
HD = D // H
NW = 125
T = 34
CAP = P * T
GT = 4
GROUPS = [(a, min(GT, T - a)) for a in range(0, T, GT)]
NG = len(GROUPS)
ZC = D + H
NT = 2
STEP = 15
FAR = 2.0 ** 100
TINY = 1e-30
EPS = 1e-5
PREP = 7
SEG_A, SEG_B, SEG_C = 3, 3, 10
SEG = SEG_A + SEG_B + SEG_C
FA = 9
FIN_READ = 5
FIN = FA + 1
NCONST = 11
VCONST = 11
XPARTS = 5
ROW_PARTS = [(0, 112), (112, NW)]
LN2 = 0.6931471805599453
ZMAX = 20.0


def gat_kernel(nc, x, src, dst, edges, ws_k, ws_b, wr_k, wr_b, we_k, we_b, attn_w, attn_b, out):
    N = x.shape[0]
    E = edges.shape[0]
    W = N // NW
    EP = E // NW
    NS = EP // STEP
    assert N == W * NW and E == NW * EP and EP == NS * STEP and W % 2 == 0
    XN = W // XPARTS

    ctx = ExitStack()
    with ctx:
        def sb(name, shape, dt=F32):
            return ctx.enter_context(nc.sbuf_tensor(name, shape, dt))

        def sem(name):
            return ctx.enter_context(nc.semaphore(name))

        xs_dram = nc.dram_tensor("xs_table", [N, D], F32).ap()

        edge_buf = sb("edge_buf", [P, 2, T, D])
        gath = sb("gath", [P, 2, T, D])
        Z = sb("Z", [P, 2, T * ZC])
        Zv = Z[:, :, :].rearrange("p b (t c) -> p b t c", c=ZC)
        onehot = sb("onehot", [P, 2, T * NW])
        OHv = onehot[:, :, :].rearrange("p b (t n) -> p b t n", n=NW)
        XR = sb("XR", [NW, W, D])
        tbuf = sb("tbuf", [P, NT, GT * D])
        edgeT = sb("edgeT", [P, 2, GT, P])
        onehotT = sb("onehotT", [NW, 2, GT, P])
        src_i = sb("src_i", [P, 2, T], I32)
        dst_i = sb("dst_i", [P, 2, T], I32)
        local = sb("local", [P, 2, T])
        far = sb("far", [P, 2, T])
        pen = sb("pen", [P, 2, H * T + 1])
        pen_head = sb("pen_head", [P, 2, T])
        pen_tail = sb("pen_tail", [P, 2, T])
        far_ends = sb("far_ends", [P, 2, 2, H])
        logit = sb("logit", [P, 2, H, T])
        run_max = sb("run_max", [P, H, T])
        row_max = sb("row_max", [P, H, T])
        seg_max = sb("seg_max", [P, H, T])
        shifted = sb("shifted", [P, H, T])
        item_far = sb("item_far", [H, P, 2])
        item_val = sb("item_val", [H, P, 2])
        item_pen = sb("item_pen", [H, 2 * P + 1])
        item_run = sb("item_run", [H, 2 * P])
        item_max = sb("item_max", [H, 2 * P])
        ends_max = sb("ends_max", [P, 2, H])
        window_base = sb("window_base", [P, 1])
        ident = sb("ident", [P, P])
        iota_i = sb("iota_i", [P, NW], I32)
        iota_f = sb("iota_f", [P, NW])
        we_sb = sb("we_sb", [P, D])
        wsr_sb = sb("wsr_sb", [P, 2, D])
        bias_in = sb("bias_in", [NW, 3, D])
        bias_sr = sb("bias_sr", [NW, 2, D])
        attn_row = sb("attn_row", [P, H, HD])
        attn_bias = sb("attn_bias", [P, 1])
        c_one = sb("c_one", [P, 1])
        c_ln2 = sb("c_ln2", [P, 1])
        c_eps = sb("c_eps", [P, 1])
        ones = sb("ones", [P, 1])
        xT = sb("xT", [P, 2, NW])
        x_in = sb("x_in", [NW, 2, D])
        den = sb("den", [NW, H])
        has = sb("has", [NW, H])
        rden = sb("rden", [NW, H])
        att = sb("att", [NW, D])
        att2 = sb("att2", [NW, D])
        rcv = sb("rcv", [NW, D])
        y = sb("y", [NW, D])
        stats = sb("stats", [NW, 6])
        mv = sb("mv", [NW, 2])
        lnv = sb("lnv", [NW, 1])
        rstd = sb("rstd", [NW, 1])
        y_out = sb("y_out", [NW, 2, D])
        bound_i = sb("bound_i", [NW, W], I32)
        bound = sb("bound", [NW, W])
        counts = sb("counts", [NW, W])
        start_f = sb("start_f", [1, W])
        start_c = sb("start_c", [1, W])
        start_i = sb("start_i", [1, W], I32)

        flatZ = Z[:, :, :].rearrange("p b f -> p (b f)")
        x_all = flatZ[0:NW, 0:W * D].rearrange("p (w d) -> p w d", d=D)
        dst_all = flatZ[0:NW, W * D:W * D + EP].bitcast(I32)
        flatOH = onehot[:, :, :].rearrange("p b f -> p (b f)")
        xs_stage = flatOH[0:NW, 0:W * D].rearrange("p (w d) -> p w d", d=D)
        below = gath[0:NW, 1, :, :].rearrange("p t d -> p (t d)").bitcast(BF16)[:, 0:W * NS]\
            .rearrange("p (w s) -> p w s", s=NS)

        def ps(name, shape):
            return ctx.enter_context(nc.psum_tensor(name, shape, F32))

        ps_edgeT = [ps(f"ps_edgeT{i}", [P, GT, P]) for i in range(2)]
        ps_onehotT = [ps(f"ps_onehotT{i}", [P, GT, P]) for i in range(2)]
        ps_z = [ps(f"ps_z{i}", [P, GT, D]) for i in range(2)]
        ps_sum = ps("ps_sum", [P, 512])
        ps_ends = ps("ps_ends", [P, 512])

        s_const = sem("s_const")
        s_xall = [sem(f"s_xall{i}") for i in range(XPARTS)]
        s_dall = sem("s_dall")
        s_pool = sem("s_pool")
        s_vconst = sem("s_vconst")
        s_xT_ps = sem("s_xT_ps")
        s_xT = sem("s_xT")
        s_xsr_ps = sem("s_xsr_ps")
        s_xsr = sem("s_xsr")
        s_table = sem("s_table")
        s_search = sem("s_search")
        s_count = sem("s_count")
        s_start = sem("s_start")
        edge_landed = [sem(f"edge_landed{b}") for b in range(2)]
        src_landed = [sem(f"src_landed{b}") for b in range(2)]
        dst_landed = [sem(f"dst_landed{b}") for b in range(2)]
        x_landed = [sem(f"x_landed{b}") for b in range(2)]
        gath_landed = [[sem(f"gath_landed{b}_{g}") for g in range(NG)] for b in range(2)]
        prep = sem("prep")
        onehot_ready = sem("onehot_ready")
        edgeT_ps = sem("edgeT_ps")
        onehotT_ps = sem("onehotT_ps")
        edgeT_ready = sem("edgeT_ready")
        onehotT_ready = sem("onehotT_ready")
        z_ps = sem("z_ps")
        z_ready = sem("z_ready")
        clamped = sem("clamped")
        exp_done = sem("exp_done")
        sq_done = sem("sq_done")
        ln_done = sem("ln_done")
        ratio_ready = sem("ratio_ready")
        mish_ready = sem("mish_ready")
        scored = sem("scored")
        logit_ready = sem("logit_ready")
        seg = sem("seg")
        ends_ps = sem("ends_ps")
        items_ready = sem("items_ready")
        back_ps = sem("back_ps")
        w_ready = sem("w_ready")
        msg_ready = sem("msg_ready")
        sum_ready = sem("sum_ready")
        fin = sem("fin")
        rstd_step = sem("rstd_step")
        stored = [sem(f"stored{b}") for b in range(2)]
        past_sp, past_pool = sem("past_sp"), sem("past_pool")
        past_pe, past_dve = sem("past_pe"), sem("past_dve")

        def at(w, g):
            return w * NG + g + 1

        def wait(eng, s, value):
            if not isinstance(value, int) or value > 0:
                eng.wait_ge(s, value)

        def wait_apart(eng, s, value, past):
            eng.wait_ge(s, value)
            eng.sem_inc(past, 1)

        def there(w):
            return not isinstance(w, int) or 0 <= w < W

        def after(w, b, g):
            return (w, b, g + 1) if g + 1 < NG else (w + 1, 1 - b, 0)

        def before(w, b, g):
            return (w, b, g - 1) if g else (w - 1, 1 - b, NG - 1)

        def run(eng, window):
            window(0, 0, 0)
            window(1, 1, 0)
            with eng.Fori(1, W // 2 - 1) as i:
                window(i * 2, 0, i)
                window(i * 2 + 1, 1, i)
            window(W - 2, 0, W // 2 - 1)
            window(W - 1, 1, W // 2 - 1)
            window(W, 0, W // 2)
            window(W + 1, 1, W // 2)

        block = ctx.enter_context(nc.Block())

        @block.sync
        def _(sp):
            def load_edges(b, start):
                sp.dma_start(edge_buf[:, b, :, :],
                             edges[bass.ds(start, CAP), :].rearrange("(p t) d -> p t d", t=T))\
                    .then_inc(edge_landed[b], 16)

            def load_indices(b, start):
                sp.dma_start(src_i[:, b, :], src[bass.ds(start, CAP)].rearrange("(p t) -> p t", t=T))\
                    .then_inc(src_landed[b], 16)
                sp.dma_start(dst_i[:, b, :], dst[bass.ds(start, CAP)].rearrange("(p t) -> p t", t=T))\
                    .then_inc(dst_landed[b], 16)

            def load_x(w, b):
                sp.dma_start(x_in[:, b, :], x[bass.ds(w * NW, NW), :]).then_inc(x_landed[b], 16)

            def store(w, b):
                wait_apart(sp, fin, w * FIN + FIN, past_sp)
                sp.dma_start(out[bass.ds(w * NW, NW), :], y_out[:, b, :]).then_inc(stored[b], 16)

            def load(w, b):
                start = sp.value_load(start_i[0:1, bass.ds(w, 1)], min_val=0, max_val=E - CAP)
                wait_apart(sp, edgeT_ps, at(w - 2, NG - 1), past_sp)
                load_edges(b, start)
                wait_apart(sp, z_ready, at(w - 2, NG - 1), past_sp)
                wait_apart(sp, prep, (w - 1) * PREP, past_sp)
                load_indices(b, start)

            sp.dma_start(wsr_sb[:, 0, :], ws_k.rearrange("f h d -> f (h d)")).then_inc(s_const, 16)
            sp.dma_start(wsr_sb[:, 1, :], wr_k.rearrange("f h d -> f (h d)")).then_inc(s_const, 16)
            xw = x.rearrange("(w p) d -> p w d", p=NW)
            for c in range(XPARTS):
                for lo, hi in ROW_PARTS:
                    sp.dma_start(x_all[lo:hi, c * XN:(c + 1) * XN, :], xw[lo:hi, c * XN:(c + 1) * XN, :])\
                        .then_inc(s_xall[c], 16)
            for k, bias in enumerate((ws_b, we_b, wr_b)):
                sp.dma_start(bias_in[:, k, :], bias.rearrange("(o h) d -> o (h d)", o=1).to_broadcast([NW, D]))\
                    .then_inc(s_const, 16)
            sp.dma_start(we_sb[:, :], we_k.rearrange("f h d -> f (h d)")).then_inc(s_const, 16)
            for h in range(H):
                sp.dma_start(attn_row[:, h, :], attn_w.rearrange("d o -> o d").to_broadcast([P, HD]))\
                    .then_inc(s_const, 16)
            sp.dma_start(attn_bias[:, :], attn_b.rearrange("(a b) -> a b", a=1).to_broadcast([P, 1]))\
                .then_inc(s_const, 16)
            load_indices(0, 0)
            load_edges(0, 0)
            sp.dma_start(dst_all, dst.rearrange("(p j) -> p j", j=EP)).then_inc(s_dall, 16)
            load_x(0, 0)
            load_x(1, 1)
            tw = xs_dram.rearrange("(w p) d -> p w d", p=NW)
            for c in range(XPARTS):
                sp.wait_ge(s_xsr, 2 * XN * (c + 1))
                for lo, hi in ROW_PARTS:
                    sp.dma_start(tw[lo:hi, c * XN:(c + 1) * XN, :], xs_stage[lo:hi, c * XN:(c + 1) * XN, :])\
                        .then_inc(s_table, 16)
            sp.wait_ge(s_start, 1)
            start = sp.value_load(start_i[0:1, 1:2], min_val=0, max_val=E - CAP)
            load_edges(1, start)
            load_indices(1, start)
            load(2, 0)
            load(3, 1)
            store(0, 0)
            load_x(2, 0)
            with sp.Fori(2, W // 2) as i:
                load(i * 2, 0)
                store(i * 2 - 3, 1)
                load_x(i * 2 - 1, 1)
                load(i * 2 + 1, 1)
                store(i * 2 - 2, 0)
                load_x(i * 2, 0)
            store(W - 3, 1)
            load_x(W - 1, 1)
            store(W - 2, 0)
            store(W - 1, 1)
            for b in range(2):
                sp.wait_ge(stored[b], 16 * (W // 2))

        @block.gpsimd
        def _(pool):
            nc.gpsimd.memset(ident[:, :], 0.0).then_inc(s_pool, 1)
            pool.wait_ge(s_pool, 1)
            nc.gpsimd.affine_select(out=ident[:, :], in_=ident[:, :], compare_op=ALU.not_equal, fill=1.0,
                                    base=0, pattern=[[-1, P]], channel_multiplier=1).then_inc(s_pool, 1)
            nc.gpsimd.iota(iota_i[:, :], pattern=[[1, NW]], base=0, channel_multiplier=0).then_inc(s_pool, 1)
            nc.gpsimd.iota(bound_i[:, :], pattern=[[NW, W]], base=0, channel_multiplier=0).then_inc(s_pool, 1)

            def gathers(b):
                for g, (a, n) in enumerate(GROUPS):
                    for t in range(a, a + n):
                        nc.gpsimd.indirect_dma_start(
                            gath[:, b, t, :], None, xs_dram,
                            bass.IndirectOffsetOnAxis(ap=src_i[:, b, t:t + 1], axis=0))\
                            .then_inc(gath_landed[b][g], 16)

            pool.wait_ge(s_table, 16 * 2 * XPARTS)
            pool.wait_ge(src_landed[0], 16)
            gathers(0)
            pool.wait_ge(s_search, 3)
            pool.wait_ge(src_landed[1], 16)
            gathers(1)
            with pool.Fori(1, W // 2) as i:
                for b in range(2):
                    pool.wait_ge(src_landed[b], i * 16 + 16)
                    wait_apart(pool, z_ready, at(i * 2 + b - 2, NG - 1), past_pool)
                    gathers(b)

        @block.tensor
        def _(pe):
            def turn_x(w):
                pe.wait_ge(s_xall[w // XN], 32)
                wait(pe, s_xT, w - 1)
                nc.tensor.transpose(ps_edgeT[w % 2][:, 0, 0:NW], x_all[:, w, :], ident[0:NW, 0:NW])\
                    .then_inc(s_xT_ps, 1)

            pe.wait_ge(s_pool, 2)
            pe.wait_ge(s_const, 16 * NCONST)
            turn_x(0)
            for w in range(W):
                if w + 1 < W:
                    turn_x(w + 1)
                pe.wait_ge(s_xT, w + 1)
                wait(pe, s_xsr, 2 * (w - 1))
                nc.tensor.matmul(ps_onehotT[w % 2][0:NW, 0:2, :], xT[:, w % 2, :], wsr_sb[:, :, :],
                                 start=True, stop=True).then_inc(s_xsr_ps, 1)
            pe.wait_ge(s_search, 3)
            nc.tensor.matmul(ps_ends[0:1, 0:W], ones[0:NW, 0:1], counts[:, :], start=True, stop=True)\
                .then_inc(s_count, 1)

            def turn(w, b, k, g):
                a, n = GROUPS[g]
                q = (b + g) % 2
                if g == 0:
                    pe.wait_ge(edge_landed[b], k * 16 + 16)
                wait(pe, edgeT_ready, at(w, g) - 2)
                for j in range(n):
                    tr = nc.tensor.transpose(ps_edgeT[q][:, j, :], edge_buf[:, b, a + j, :], ident[:, :])
                tr.then_inc(edgeT_ps, 1)
                pe.wait_ge(onehot_ready, at(w, g))
                wait(pe, onehotT_ready, at(w, g) - 2)
                for j in range(n):
                    tr = nc.tensor.transpose(ps_onehotT[q][0:NW, j, :], OHv[:, b, a + j, :], ident[:, :])
                tr.then_inc(onehotT_ps, 1)

            def products(w, b, g):
                a, n = GROUPS[g]
                q = (b + g) % 2
                pe.wait_ge(edgeT_ready, at(w, g))
                pe.wait_ge(onehotT_ready, at(w, g))
                wait(pe, z_ready, at(w, g) - 2)
                for j in range(n):
                    nc.tensor.matmul(ps_z[q][:, j, :], edgeT[:, q, j, :], we_sb[:, :], start=True, stop=False)
                    mm = nc.tensor.matmul(ps_z[q][:, j, :], onehotT[:, q, j, :], XR[:, bass.ds(w, 1), :],
                                          start=False, stop=True)
                mm.then_inc(z_ps, 1)

            def sums(w, b, g):
                a, n = GROUPS[g]
                if g == 0:
                    wait(pe, fin, (w - 1) * FIN + FIN_READ)
                pe.wait_ge(msg_ready, at(w, g))
                for t in range(a, a + n):
                    mm = nc.tensor.matmul(ps_sum[0:NW, 0:ZC], OHv[:, b, t, :], Zv[:, b, t, :],
                                          start=(t == 0), stop=(t == T - 1))
                mm.then_inc(sum_ready, 1)

            def ends_to_row(w, b):
                pe.wait_ge(seg, w * SEG + SEG_A)
                for c, ends in enumerate((row_max[:, :, 0], row_max[:, :, T - 1],
                                          far_ends[:, b, 0, :], far_ends[:, b, 1, :])):
                    tr = nc.tensor.transpose(ps_ends[0:H, c * P:(c + 1) * P], ends, ident[:, :])
                tr.then_inc(ends_ps, 1)

            def maxima_back(w):
                wait_apart(pe, seg, w * SEG + SEG_A + SEG_B, past_pe)
                im = item_max[:, :].rearrange("h (p k) -> h k p", k=2)
                for c in range(2):
                    tr = nc.tensor.transpose(ps_ends[:, c * H:(c + 1) * H], im[:, c, :], ident[0:H, 0:H])
                tr.then_inc(back_ps, 1)

            def window(w, b, k):
                for g in range(NG):
                    if there(w):
                        products(w, b, g)
                    w1, b1, g1 = after(w, b, g)
                    if there(w1) and there(w):
                        turn(w1, b1, k if w1 is w else (k + b if b else k), g1)
                    if g == 0 and there(w - 2):
                        sums(w - 2, b, NG - 1)
                    if g == 1 and there(w - 1):
                        ends_to_row(w - 1, 1 - b)
                    if g == 3 and there(w - 1):
                        maxima_back(w - 1)
                    if g >= 5 and there(w - 1):
                        for m in (2 * (g - 5), 2 * (g - 5) + 1):
                            sums(w - 1, 1 - b, m)

            turn(0, 0, 0, 0)
            run(pe, window)

        @block.scalar
        def _(act):
            nc.scalar.preload_act_table_set("natural_log_exp_and_others")
            for w in range(W):
                act.wait_ge(s_xT_ps, w + 1)
                wait(act, s_xsr_ps, w - 1)
                nc.scalar.copy(xT[:, w % 2, :], ps_edgeT[w % 2][:, 0, 0:NW]).then_inc(s_xT, 1)
            act.wait_ge(s_vconst, VCONST)

            def copies(w, b, g):
                n = GROUPS[g][1]
                q = (b + g) % 2
                act.wait_ge(edgeT_ps, at(w, g))
                wait(act, z_ps, at(w, g) - 2)
                nc.scalar.copy(edgeT[:, q, 0:n, :], ps_edgeT[q][:, 0:n, :]).then_inc(edgeT_ready, 1)
                act.wait_ge(onehotT_ps, at(w, g))
                nc.scalar.copy(onehotT[:, q, 0:n, :], ps_onehotT[q][0:NW, 0:n, :]).then_inc(onehotT_ready, 1)

            def ratio(w, b, g):
                n = GROUPS[g][1]
                tb = tbuf[:, (b + g) % 2, 0:n * D]
                act.wait_ge(clamped, at(w, g))
                nc.scalar.activation(tb, tb, ACT.Exp).then_inc(exp_done, 1)
                act.wait_ge(exp_done, at(w, g))
                nc.scalar.activation(tb, tb, ACT.Square, bias=c_one[:, 0:1]).then_inc(sq_done, 1)
                act.wait_ge(sq_done, at(w, g))
                nc.scalar.activation(tb, tb, ACT.Ln, bias=c_one[:, 0:1]).then_inc(ln_done, 1)
                act.wait_ge(ln_done, at(w, g))
                nc.scalar.activation(tb, tb, ACT.Exp, bias=c_ln2[:, 0:1], scale=-1.0).then_inc(ratio_ready, 1)

            def items(w):
                act.wait_ge(ends_ps, w + 1)
                nc.scalar.copy(item_val[:, :, :].rearrange("h p k -> h k p"),
                               ps_ends[0:H, 0:2 * P].rearrange("h (k p) -> h k p", k=2)).then_inc(items_ready, 1)
                nc.scalar.copy(item_far[:, :, :].rearrange("h p k -> h k p"),
                               ps_ends[0:H, 2 * P:4 * P].rearrange("h (k p) -> h k p", k=2))\
                    .then_inc(items_ready, 1)

            def weights(w, b):
                act.wait_ge(seg, w * SEG + SEG)
                nc.scalar.activation(Zv[:, b, :, D:ZC].rearrange("p t h -> p h t"), shifted[:, :, :], ACT.Exp)\
                    .then_inc(w_ready, 1)

            def inverse_std(w):
                act.wait_ge(fin, w * FIN + FA)
                nc.scalar.activation(lnv[:, :], mv[:, 1:2], ACT.Ln, bias=c_eps[0:NW, 0:1]).then_inc(rstd_step, 1)
                act.wait_ge(rstd_step, w * 2 + 1)
                nc.scalar.activation(rstd[:, :], lnv[:, :], ACT.Exp, scale=-0.5).then_inc(rstd_step, 1)

            def window(w, b, k):
                for g in range(NG):
                    w1, b1, g1 = after(w, b, g)
                    if there(w1) and there(w):
                        copies(w1, b1, g1)
                    if there(w):
                        ratio(w, b, g)
                    if g == 1 and there(w - 1):
                        items(w - 1)
                    if g == 2 and there(w - 2):
                        inverse_std(w - 2)
                    if g == 3 and there(w - 1):
                        weights(w - 1, 1 - b)

            copies(0, 0, 0)
            run(act, window)

        @block.vector
        def _(dve):
            nc.vector.memset(c_one[:, :], 1.0).then_inc(s_vconst, 1)
            nc.vector.memset(c_ln2[:, :], LN2).then_inc(s_vconst, 1)
            nc.vector.memset(c_eps[:, :], EPS).then_inc(s_vconst, 1)
            nc.vector.memset(ones[:, :], 1.0).then_inc(s_vconst, 1)
            nc.vector.memset(pen[:, :, :], -FAR).then_inc(s_vconst, 1)
            nc.vector.memset(item_pen[:, :], -FAR).then_inc(s_vconst, 1)
            nc.vector.memset(window_base[:, :], -float(NW)).then_inc(s_vconst, 1)
            dve.wait_ge(s_pool, 4)
            nc.vector.tensor_copy(iota_f[:, :], iota_i[:, :]).then_inc(s_vconst, 1)
            nc.vector.tensor_copy(bound[:, :], bound_i[:, :]).then_inc(s_vconst, 1)
            dve.wait_ge(s_const, 16 * NCONST)
            nc.vector.tensor_tensor(bias_sr[:, 0, :], bias_in[:, 0, :], bias_in[:, 1, :], ALU.add)\
                .then_inc(s_vconst, 1)
            nc.vector.tensor_copy(bias_sr[:, 1, :], bias_in[:, 2, :]).then_inc(s_vconst, 1)
            dve.wait_ge(s_vconst, VCONST)
            for w in range(W):
                dve.wait_ge(s_xsr_ps, w + 1)
                nc.vector.tensor_tensor(xs_stage[:, w, :], ps_onehotT[w % 2][0:NW, 0, :], bias_sr[:, 0, :],
                                        ALU.add).then_inc(s_xsr, 1)
                nc.vector.tensor_tensor(XR[:, w, :], ps_onehotT[w % 2][0:NW, 1, :], bias_sr[:, 1, :],
                                        ALU.add).then_inc(s_xsr, 1)

            dve.wait_ge(s_dall, 16)
            seen = dst_all.rearrange("p (s k) -> p s k", k=STEP)[:, :, 0]
            nc.vector.tensor_tensor(below, seen.unsqueeze(1).to_broadcast([NW, W, NS]),
                                    bound[:, :].unsqueeze(2).to_broadcast([NW, W, NS]), ALU.is_lt)\
                .then_inc(s_search, 1)
            dve.wait_ge(s_search, 1)
            nc.vector.tensor_reduce(counts[:, :], below, AX.X, ALU.add).then_inc(s_search, 2)
            dve.wait_ge(s_count, 1)
            nc.vector.tensor_scalar(start_f[:, :], ps_ends[0:1, 0:W], float(STEP), -float(STEP), ALU.mult,
                                    ALU.add).then_inc(s_search, 1)
            dve.wait_ge(s_search, 4)
            nc.vector.tensor_scalar(start_i[:, :], start_f[:, :], 0.0, float(E - CAP), ALU.max, ALU.min)\
                .then_inc(s_start, 1)

            def prepare(w, b, k):
                base = w * PREP
                dve.wait_ge(dst_landed[b], k * 16 + 16)
                nc.vector.tensor_scalar(window_base[:, :], window_base[:, :], float(NW), None, ALU.add)\
                    .then_inc(prep, 1)
                dve.wait_ge(prep, base + 1)
                nc.vector.tensor_scalar(local[:, b, :], dst_i[:, b, :], window_base[:, 0:1], None, ALU.subtract)\
                    .then_inc(prep, 1)
                nc.vector.tensor_scalar(far[:, b, :], dst_i[:, b, :], FAR, None, ALU.mult).then_inc(prep, 1)
                dve.wait_ge(prep, base + 3)
                f = far[:, b, :].unsqueeze(1)
                nc.vector.tensor_tensor(pen[:, b, 0:H * T].rearrange("p (h t) -> p h t", t=T)[:, :, 1:T],
                                        f[:, :, 0:T - 1].to_broadcast([P, H, T - 1]),
                                        f[:, :, 1:T].to_broadcast([P, H, T - 1]), ALU.subtract).then_inc(prep, 1)
                nc.vector.tensor_scalar(pen_head[:, b, :], far[:, b, :], far[:, b, 0:1], -1.0, ALU.subtract,
                                        ALU.mult).then_inc(prep, 1)
                nc.vector.tensor_scalar(pen_tail[:, b, :], far[:, b, :], far[:, b, T - 1:T], None,
                                        ALU.subtract).then_inc(prep, 1)
                nc.vector.tensor_copy(far_ends[:, b, :, :],
                                      far[:, b, 0:T:T - 1].unsqueeze(2).to_broadcast([P, 2, H])).then_inc(prep, 1)

            def one_hots(w, b, g):
                a, n = GROUPS[g]
                wait(dve, sum_ready, at(w - 2, g))
                dve.wait_ge(prep, w * PREP + 2)
                nc.vector.tensor_tensor(OHv[:, b, a:a + n, :],
                                        iota_f[:, :].unsqueeze(1).to_broadcast([P, n, NW]),
                                        local[:, b, a:a + n].unsqueeze(2).to_broadcast([P, n, NW]),
                                        ALU.is_equal).then_inc(onehot_ready, 1)

            def add_gathered(w, b, k, g):
                a, n = GROUPS[g]
                dve.wait_ge(z_ps, at(w, g))
                dve.wait_ge(gath_landed[b][g], k * (16 * n) + 16 * n)
                nc.vector.tensor_tensor(Zv[:, b, a:a + n, 0:D], ps_z[(b + g) % 2][:, 0:n, :],
                                        gath[:, b, a:a + n, :], ALU.add).then_inc(z_ready, 1)

            def clamp(w, b, g):
                a, n = GROUPS[g]
                dve.wait_ge(z_ready, at(w, g))
                tb = tbuf[:, (b + g) % 2, 0:n * D].rearrange("p (t d) -> p t d", d=D)
                nc.vector.tensor_scalar(tb, Zv[:, b, a:a + n, 0:D], ZMAX, None, ALU.min).then_inc(clamped, 1)

            def mish(w, b, g):
                a, n = GROUPS[g]
                dve.wait_ge(ratio_ready, at(w, g))
                tb = tbuf[:, (b + g) % 2, 0:n * D].rearrange("p (t d) -> p t d", d=D)
                nc.vector.scalar_tensor_tensor(out=tb, in0=tb, scalar=1.0, in1=Zv[:, b, a:a + n, 0:D],
                                               op0=ALU.subtract, op1=ALU.mult, reverse0=True)\
                    .then_inc(mish_ready, 1)

            def score(w, b, g):
                n = GROUPS[g][1]
                dve.wait_ge(mish_ready, at(w, g))
                tb = tbuf[:, (b + g) % 2, 0:n * D].rearrange("p (t d) -> p t d", d=D)
                row = attn_row[:, :, :].rearrange("p h d -> p (h d)").unsqueeze(1)
                nc.vector.tensor_tensor(tb, tb, row.to_broadcast([P, n, D]), ALU.mult).then_inc(scored, 1)

            def reduce_heads(w, b, g):
                a, n = GROUPS[g]
                dve.wait_ge(scored, at(w, g))
                tb = tbuf[:, (b + g) % 2, 0:n * D].rearrange("p (t h d) -> p t h d", h=H, d=HD)
                nc.vector.tensor_reduce(logit[:, b, :, a:a + n].rearrange("p h t -> p t h"), tb, AX.X, ALU.add)\
                    .then_inc(logit_ready, 1)

            def maxima_in_partitions(w, b):
                base = w * SEG
                lg = logit[:, b, :, :].rearrange("p h t -> p (h t)")
                run_ = run_max[:, :, :].rearrange("p h t -> p (h t)")
                row_ = row_max[:, :, :].rearrange("p h t -> p (h t)")
                dve.wait_ge(logit_ready, at(w, NG - 1))
                nc.vector.tensor_scalar(lg, lg, attn_bias[:, 0:1], None, ALU.add).then_inc(seg, 1)
                dve.wait_ge(seg, base + 1)
                nc.vector.tensor_tensor_scan(run_, pen[:, b, 0:H * T], lg, 0.0, ALU.add, ALU.max).then_inc(seg, 1)
                dve.wait_ge(seg, base + 2)
                nc.vector.tensor_tensor_scan(row_[:, ::-1], pen[:, b, 1:H * T + 1][:, ::-1], run_[:, ::-1], 0.0,
                                             ALU.add, ALU.max).then_inc(seg, 1)

            def maxima_over_partitions(w):
                base = w * SEG + SEG_A
                dve.wait_ge(items_ready, w * 2 + 2)
                far_ = item_far[:, :, :].rearrange("h p k -> h (p k)")
                val_ = item_val[:, :, :].rearrange("h p k -> h (p k)")
                nc.vector.tensor_tensor(item_pen[:, 1:2 * P], far_[:, 0:2 * P - 1], far_[:, 1:2 * P],
                                        ALU.subtract).then_inc(seg, 1)
                dve.wait_ge(seg, base + 1)
                nc.vector.tensor_tensor_scan(item_run[:, :], item_pen[:, 0:2 * P], val_, 0.0, ALU.add, ALU.max)\
                    .then_inc(seg, 1)
                dve.wait_ge(seg, base + 2)
                nc.vector.tensor_tensor_scan(item_max[:, ::-1], item_pen[:, 1:2 * P + 1][:, ::-1],
                                             item_run[:, ::-1], 0.0, ALU.add, ALU.max).then_inc(seg, 1)

            def subtract_maxima(w, b):
                base = w * SEG + SEG_A + SEG_B
                dve.wait_ge(back_ps, w + 1)
                nc.vector.tensor_copy(ends_max[:, :, :].rearrange("p k h -> p (k h)"), ps_ends[:, 0:2 * H])\
                    .then_inc(seg, 1)
                dve.wait_ge(seg, base + 1)
                for h in range(H):
                    nc.vector.scalar_tensor_tensor(out=seg_max[:, h, :], in0=pen_head[:, b, :],
                                                   scalar=ends_max[:, 0, h:h + 1], in1=row_max[:, h, :],
                                                   op0=ALU.add, op1=ALU.max).then_inc(seg, 1)
                dve.wait_ge(seg, base + 1 + H)
                for h in range(H):
                    nc.vector.scalar_tensor_tensor(out=seg_max[:, h, :], in0=pen_tail[:, b, :],
                                                   scalar=ends_max[:, 1, h:h + 1], in1=seg_max[:, h, :],
                                                   op0=ALU.add, op1=ALU.max).then_inc(seg, 1)
                dve.wait_ge(seg, base + 1 + 2 * H)
                nc.vector.tensor_tensor(shifted[:, :, :], logit[:, b, :, :], seg_max[:, :, :], ALU.subtract)\
                    .then_inc(seg, 1)

            def messages(w, b, g):
                a, n = GROUPS[g]
                dve.wait_ge(w_ready, w + 1)
                zz = Zv[:, b, a:a + n, 0:D].rearrange("p t (h d) -> p t h d", h=H)
                ww = Zv[:, b, a:a + n, D:ZC].unsqueeze(3).to_broadcast([P, n, H, HD])
                nc.vector.tensor_tensor(zz, zz, ww, ALU.mult).then_inc(msg_ready, 1)

            def attended(w, b, k):
                base = w * FIN
                heads = lambda ap: ap.rearrange("p (h d) -> p h d", h=H)
                wide = lambda ap: ap.unsqueeze(2).to_broadcast([NW, H, HD])
                dve.wait_ge(sum_ready, at(w, NG - 1))
                nc.vector.tensor_scalar(den[:, :], ps_sum[0:NW, D:ZC], TINY, None, ALU.max).then_inc(fin, 1)
                nc.vector.tensor_scalar(has[:, :], ps_sum[0:NW, D:ZC], 0.0, None, ALU.is_gt).then_inc(fin, 1)
                dve.wait_ge(fin, base + 2)
                nc.vector.reciprocal(rden[:, :], den[:, :]).then_inc(fin, 1)
                nc.vector.tensor_tensor(heads(rcv[:, :]), heads(XR[:, bass.ds(w, 1), :].rearrange("p o d -> p (o d)")),
                                        wide(has[:, :]), ALU.mult).then_inc(fin, 1)
                dve.wait_ge(fin, base + 4)
                nc.vector.tensor_tensor(heads(att[:, :]), heads(ps_sum[0:NW, 0:D]), wide(rden[:, :]), ALU.mult)\
                    .then_inc(fin, 1)
                dve.wait_ge(fin, base + 5)
                nc.vector.tensor_tensor(att2[:, :], att[:, :], rcv[:, :], ALU.subtract).then_inc(fin, 1)
                dve.wait_ge(x_landed[b], k * 16 + 16)
                dve.wait_ge(fin, base + 6)
                nc.vector.tensor_tensor(y[:, :], att2[:, :], x_in[:, b, :], ALU.add).then_inc(fin, 1)
                dve.wait_ge(fin, base + 7)
                nc.vector.bn_stats(stats[:, :], y[:, :]).then_inc(fin, 1)
                wait_apart(dve, fin, base + 8, past_dve)
                nc.vector.bn_aggr(mv[:, :], stats[:, :]).then_inc(fin, 1)

            def normalise(w, b, k):
                dve.wait_ge(rstd_step, w * 2 + 2)
                wait(dve, stored[b], k * 16)
                nc.vector.tensor_scalar(y_out[:, b, :], y[:, :], mv[:, 0:1], rstd[:, 0:1], ALU.subtract, ALU.mult)\
                    .then_inc(fin, 1)

            def window(w, b, k):
                for g in range(NG):
                    w1, b1, g1 = after(w, b, g)
                    w0, b0, g0 = before(w, b, g)
                    if there(w1) and there(w):
                        one_hots(w1, b1, g1)
                    if there(w):
                        add_gathered(w, b, k, g)
                    if there(w0):
                        mish(w0, b0, g0)
                    if there(w):
                        clamp(w, b, g)
                    if there(w0):
                        score(w0, b0, g0)
                    if g >= 4 and there(w - 1):
                        messages(w - 1, 1 - b, 2 * (g - 4))
                    if there(w0):
                        reduce_heads(w0, b0, g0)
                    if 4 <= g < NG - 1 and there(w - 1):
                        messages(w - 1, 1 - b, 2 * (g - 4) + 1)
                    if g == 0 and there(w - 1):
                        maxima_in_partitions(w - 1, 1 - b)
                    if g == 1 and there(w - 2):
                        attended(w - 2, b, k - 1)
                    if g == 2 and there(w - 1):
                        maxima_over_partitions(w - 1)
                    if g == 3 and there(w - 1):
                        subtract_maxima(w - 1, 1 - b)
                    if g == 4 and there(w - 2):
                        normalise(w - 2, b, k - 1)
                    if g == 7 and there(w + 1) and there(w):
                        prepare(w + 1, 1 - b, k + b if b else k)

            prepare(0, 0, 0)
            dve.wait_ge(s_table, 16 * 2 * XPARTS)
            one_hots(0, 0, 0)
            run(dve, window)


_INS = ["x", "src", "dst", "edge_attr_128", "L0_gnn_Ws_k", "L0_gnn_Ws_b", "L0_gnn_Wr_k", "L0_gnn_Wr_b",
        "L0_gnn_We_k", "L0_gnn_We_b", "L0_gnn_attn_w", "L0_gnn_attn_b"]


def kernel(**inputs):
    import numpy as _np
    import concourse.bacc as _bacc
    from concourse import mybir as _mybir
    from concourse.bass_utils import run_bass_kernel_spmd as _run

    nc = _bacc.Bacc("TRN2", target_bir_lowering=False, num_devices=1)
    arrays, args = {}, []
    for name in _INS:
        a = _np.ascontiguousarray(inputs[name])
        arrays[f"in_{name}_dram"] = a
        args.append(nc.dram_tensor(f"in_{name}_dram", a.shape, _mybir.dt.from_np(a.dtype), kind="ExternalInput").ap())
    shape = tuple(inputs["x"].shape)
    args.append(nc.dram_tensor("out_0_dram", shape, _mybir.dt.float32, kind="ExternalOutput").ap())
    gat_kernel(nc, *args)
    r = _run(nc, [arrays], core_ids=[0])
    return r.results[0]["out_0_dram"]
```

```python
from contextlib import ExitStack

import concourse.bass as bass
from concourse import mybir

F32 = mybir.dt.float32
I32 = mybir.dt.int32
BF16 = mybir.dt.bfloat16
ALU = mybir.AluOpType
ACT = mybir.ActivationFunctionType
AX = mybir.AxisListType

P = 128
D = 128
H = 4
HD = D // H
NW = 125
T = 34
CAP = P * T
GT = 4
GROUPS = [(a, min(GT, T - a)) for a in range(0, T, GT)]
NG = len(GROUPS)
ZC = D + H
NT = 3
TURNED = [2, 3, 4, 5, 6]
TURN_T = 3
STEP = 15
FAR = 2.0 ** 100
TINY = 1e-30
EPS = 1e-5
PREP = 7
SEG_A, SEG_B, SEG_C = 3, 3, 5
ENDS_READ = 2
SEG = SEG_A + SEG_B + SEG_C
FA = 9
FIN_READ = 5
FIN = FA + 1
MSG_NEXT = {4: [0, 1], 5: [2], 6: [3], 7: [4], 8: [5]}
MSG_LAST = {0: [6], 1: [7], 2: [8]}
SUM_NEXT = {5: [0], 6: [1], 7: [2], 8: [3]}
SUM_LAST = {0: [4, 5], 1: [6], 2: [7], 3: [8]}
NCONST = 5
NLATER = 10
VCONST = 13
BOUNDS = 11
SEARCH = 5
FLAG = 7
XPARTS = 5
ROW_PARTS = [(0, 112), (112, NW)]
LN2 = 0.6931471805599453
ZMAX = 20.0


def gat_kernel(nc, x, src, dst, edges, ws_k, ws_b, wr_k, wr_b, we_k, we_b, attn_w, attn_b, out):
    N = x.shape[0]
    E = edges.shape[0]
    W = N // NW
    EP = E // NW
    NS = EP // STEP
    assert N == W * NW and E == NW * EP and EP == NS * STEP and W % 2 == 0
    XN = W // XPARTS

    ctx = ExitStack()
    with ctx:
        def sb(name, shape, dt=F32):
            return ctx.enter_context(nc.sbuf_tensor(name, shape, dt))

        def sem(name):
            return ctx.enter_context(nc.semaphore(name))

        xs_dram = nc.dram_tensor("xs_table", [N, D], F32).ap()
        xr_dram = nc.dram_tensor("xr_table", [N, D], F32).ap()
        max_dram = nc.dram_tensor("max_table", [N + NW, H], F32).ap()
        acc_dram = nc.dram_tensor("acc_table", [N + NW, ZC], F32).ap()
        z_dram = nc.dram_tensor("z_rows", [E, D], F32).ap()
        logit_dram = nc.dram_tensor("logit_rows", [E, H], F32).ap()

        edge_buf = sb("edge_buf", [P, 2, T, D])
        gath = sb("gath", [P, 2, T, D])
        Z = sb("Z", [P, 2, T * ZC])
        Zv = Z[:, :, :].rearrange("p b (t c) -> p b t c", c=ZC)
        onehot = sb("onehot", [P, 2, T * NW])
        OHv = onehot[:, :, :].rearrange("p b (t n) -> p b t n", n=NW)
        XR = sb("XR", [NW, W, D])
        tbuf = sb("tbuf", [P, NT, GT * D])
        edgeT = sb("edgeT", [P, 2, GT, P])
        onehotT = sb("onehotT", [NW, 2, GT, P])
        src_i = sb("src_i", [P, 2, T], I32)
        dst_i = sb("dst_i", [P, 2, T], I32)
        local = sb("local", [P, 2, T])
        far = sb("far", [P, 2, T])
        pen = sb("pen", [P, 2, H * T + 1])
        pen_head = sb("pen_head", [P, 2, T])
        pen_tail = sb("pen_tail", [P, 2, T])
        far_ends = sb("far_ends", [P, 2, 2, H])
        logit = sb("logit", [P, 2, H, T])
        run_max = sb("run_max", [P, H, T])
        row_max = sb("row_max", [P, H, T])
        seg_max = sb("seg_max", [P, H, T])
        shifted = sb("shifted", [P, H, T])
        item_far = sb("item_far", [H, P, 2])
        item_val = sb("item_val", [H, P, 2])
        item_pen = sb("item_pen", [H, 2 * P + 1])
        item_run = sb("item_run", [H, 2 * P])
        item_max = sb("item_max", [H, 2 * P])
        ends_max = sb("ends_max", [P, 2, H, T])
        window_base = sb("window_base", [P, 1])
        ident = sb("ident", [P, P])
        ident_half = sb("ident_half", [P, P], BF16)
        mishT = sb("mishT", [P, TURN_T, P])
        attn_cols = sb("attn_cols", [P, H])
        iota_i = sb("iota_i", [P, NW], I32)
        iota_f = sb("iota_f", [P, NW])
        we_sb = sb("we_sb", [P, D])
        wsr_sb = sb("wsr_sb", [P, 2, D])
        bias_in = sb("bias_in", [NW, 3, D])
        bias_sr = sb("bias_sr", [NW, 2, D])
        attn_row = sb("attn_row", [P, H, HD])
        attn_bias = sb("attn_bias", [P, 1])
        c_one = sb("c_one", [P, 1])
        c_ln2 = sb("c_ln2", [P, 1])
        c_eps = sb("c_eps", [P, 1])
        ones = sb("ones", [P, 1])
        xT = sb("xT", [P, 2, NW])
        x_in = sb("x_in", [NW, 2, D])
        den = sb("den", [NW, H])
        has = sb("has", [NW, H])
        rden = sb("rden", [NW, H])
        att = sb("att", [NW, D])
        att2 = sb("att2", [NW, D])
        rcv = sb("rcv", [NW, D])
        y = sb("y", [NW, D])
        stats = sb("stats", [NW, 6])
        mv = sb("mv", [NW, 2])
        lnv = sb("lnv", [NW, 1])
        rstd = sb("rstd", [NW, 1])
        y_out = sb("y_out", [NW, 2, D])
        bound_i = sb("bound_i", [NW, W], I32)
        bound = sb("bound", [NW, W])
        counts = sb("counts", [NW, W + 2])
        next_first = sb("next_first", [NW, 1], I32)
        run_end = sb("run_end", [1, W])
        late = sb("late", [1, W + 2])
        flag_f = sb("flag_f", [1, 1])
        flag_i = sb("flag_i", [1, 1], I32)
        g_small = sb("g_small", [NW, 64])
        g_index = sb("g_index", [NW, 1], I32)
        g_iota = sb("g_iota", [NW, 2], I32)
        g_down_i = sb("g_down_i", [NW, NW], I32)
        start_f = sb("start_f", [1, W])
        start_c = sb("start_c", [1, W])
        start_i = sb("start_i", [1, W], I32)

        flatZ = Z[:, :, :].rearrange("p b f -> p (b f)")
        x_all = flatZ[0:NW, 0:W * D].rearrange("p (w d) -> p w d", d=D)
        dst_all = flatZ[0:NW, W * D:W * D + EP].bitcast(I32)
        flatOH = onehot[:, :, :].rearrange("p b f -> p (b f)")
        xs_stage = flatOH[0:NW, 0:W * D].rearrange("p (w d) -> p w d", d=D)
        below = gath[0:NW, 1, :, :].rearrange("p t d -> p (t d)").bitcast(BF16)[:, 0:W * NS]\
            .rearrange("p (w s) -> p w s", s=NS)

        def ps(name, shape):
            return ctx.enter_context(nc.psum_tensor(name, shape, F32))

        ps_edgeT = [ps(f"ps_edgeT{i}", [P, GT, P]) for i in range(2)]
        ps_onehotT = [ps(f"ps_onehotT{i}", [P, GT, P]) for i in range(2)]
        ps_z = [ps(f"ps_z{i}", [P, GT, D]) for i in range(2)]
        ps_sum = ps("ps_sum", [P, 512])
        ps_ends = ps("ps_ends", [P, 512])
        ps_mishT = ps_ends[:, :].rearrange("p (t e) -> p t e", e=P)
        ps_logit = ps_ends[:, TURN_T * P:TURN_T * P + len(TURNED) * TURN_T * H]

        def halves(ap):
            return ap.bitcast(BF16)[:, 1::2]

        s_const = sem("s_const")
        s_later = sem("s_later")
        s_xall = [sem(f"s_xall{i}") for i in range(XPARTS)]
        s_dall = sem("s_dall")
        s_pool = sem("s_pool")
        s_vconst = sem("s_vconst")
        s_xT_ps = sem("s_xT_ps")
        s_xT = sem("s_xT")
        s_xsr_ps = sem("s_xsr_ps")
        s_xsr = sem("s_xsr")
        s_table = sem("s_table")
        s_search = sem("s_search")
        s_count = sem("s_count")
        s_start = sem("s_start")
        s_flag = sem("s_flag")
        s_sorted_done = sem("s_sorted_done")
        g_init = sem("g_init")
        g_made = sem("g_made")
        g_load = [[sem(f"g_load{c}{k}") for k in range(3)] for c in "ABC"]
        g_gath = [[sem(f"g_gath{c}{k}") for k in range(n)] for c, n in (("A", 3), ("B", 2))]
        g_scat = [sem(f"g_scat{c}") for c in "ABC"]
        g_pe = [sem(f"g_pe{c}") for c in "ABC"]
        g_act = [sem(f"g_act{c}") for c in "ABC"]
        g_dve = [sem(f"g_dve{c}") for c in "ABC"]
        g_store = [sem(f"g_store{c}") for c in "ABC"]
        edge_landed = [sem(f"edge_landed{b}") for b in range(2)]
        src_landed = [sem(f"src_landed{b}") for b in range(2)]
        dst_landed = [sem(f"dst_landed{b}") for b in range(2)]
        x_landed = [sem(f"x_landed{b}") for b in range(2)]
        gath_landed = [[sem(f"gath_landed{b}_{g}") for g in range(NG)] for b in range(2)]
        prep = sem("prep")
        onehot_ready = sem("onehot_ready")
        edgeT_ps = sem("edgeT_ps")
        onehotT_ps = sem("onehotT_ps")
        edgeT_ready = sem("edgeT_ready")
        onehotT_ready = sem("onehotT_ready")
        z_ps = sem("z_ps")
        z_ready = sem("z_ready")
        clamped = sem("clamped")
        exp_done = sem("exp_done")
        sq_done = sem("sq_done")
        ln_done = sem("ln_done")
        ratio_ready = sem("ratio_ready")
        mish_ready = sem("mish_ready")
        mishT_ps = sem("mishT_ps")
        mishT_ready = sem("mishT_ready")
        heads_ps = sem("heads_ps")
        heads_read = sem("heads_read")
        scored = sem("scored")
        logit_ready = sem("logit_ready")
        seg = sem("seg")
        ends_ps = sem("ends_ps")
        items_ready = sem("items_ready")
        back_ps = sem("back_ps")
        w_ready = sem("w_ready")
        msg_ready = sem("msg_ready")
        sum_ready = sem("sum_ready")
        fin = sem("fin")
        rstd_step = sem("rstd_step")
        stored = [sem(f"stored{b}") for b in range(2)]
        past_sp, past_pool = sem("past_sp"), sem("past_pool")
        past_pe, past_dve = sem("past_pe"), sem("past_dve")
        past_max, past_w = sem("past_max"), sem("past_w")

        def at(w, g):
            return w * NG + g + 1

        def at_turned(w, g):
            return w * len(TURNED) + TURNED.index(g) + 1

        def back(w, b, g, n):
            for _ in range(n):
                w, b, g = before(w, b, g)
            return w, b, g

        def wait(eng, s, value):
            if not isinstance(value, int) or value > 0:
                eng.wait_ge(s, value)

        def wait_apart(eng, s, value, past):
            eng.wait_ge(s, value)
            eng.sem_inc(past, 1)

        def there(w):
            return not isinstance(w, int) or 0 <= w < W

        def after(w, b, g):
            return (w, b, g + 1) if g + 1 < NG else (w + 1, 1 - b, 0)

        def before(w, b, g):
            return (w, b, g - 1) if g else (w - 1, 1 - b, NG - 1)

        def run(eng, window):
            window(0, 0, 0)
            window(1, 1, 0)
            with eng.Fori(1, W // 2 - 1) as i:
                window(i * 2, 0, i)
                window(i * 2 + 1, 1, i)
            window(W - 2, 0, W // 2 - 1)
            window(W - 1, 1, W // 2 - 1)
            window(W, 0, W // 2)
            window(W + 1, 1, W // 2)


        GTILES = E // NW
        g_edge = edge_buf[0:NW, 0, 0, :]
        g_xs = gath[0:NW, 0, 0, :]
        g_xr = gath[0:NW, 0, 1, :]
        g_x = gath[0:NW, 0, 2, :]
        g_acc = gath[0:NW, 0, 3:5, :].rearrange("p t d -> p (t d)")[:, 0:ZC]
        g_new = gath[0:NW, 0, 5:7, :].rearrange("p t d -> p (t d)")[:, 0:ZC]
        g_z = Z[0:NW, 0, 0:D]
        g_msg = Z[0:NW, 0, D:D + ZC]
        g_t = tbuf[0:NW, 0, 0:D]
        g_edgeT = edgeT[:, 0, 0, 0:NW]
        g_same = OHv[0:NW, 0, 0, :]
        g_bar = OHv[0:NW, 0, 1, :]
        g_down = OHv[0:NW, 0, 2, :]
        g_rank = OHv[0:NW, 0, 3, :]
        g_dst_wide = OHv[0:NW, 0, 4, :]
        g_logit_wide = OHv[0:NW, 0, 5:9, :]
        g_barred = OHv[0:NW, 0, 9:13, :]
        g_fill = OHv[0:NW, 0, 13:17, :].rearrange("p t n -> p (t n)")
        g_src = src_i[0:NW, 0, 0:1]
        g_dst = dst_i[0:NW, 0, 0:1]
        col = lambda a, n: g_small[:, a:a + n]
        g_dstf, g_self, g_trash, g_lead, g_first, g_move, g_moved = [col(c, 1) for c in range(7)]
        g_logit, g_max, g_tmax, g_newmax, g_shift, g_w, g_sum_w = [col(8 + H * c, H) for c in range(7)]
        p_edge = ps_edgeT[0][:, 0, 0:NW]
        p_z = ps_z[0][0:NW, 0, :]
        p_dst = ps_z[1][0:NW, 0, 0:NW]
        p_logit = ps_onehotT[0][0:NW, :, 0:NW]
        p_sum = ps_sum[0:NW, 0:ZC]
        KD = [21, 14, 10]
        KA = [5, 1, 2]
        KP = [3, 2, 0]

        def general(eng, path):
            eng.wait_ge(s_flag, FLAG)
            flag = eng.value_load(flag_i[0:1, 0:1], min_val=0, max_val=E)
            with eng.If(flag > 0):
                eng.wait_ge(s_sorted_done, 1)
                path(eng)

        def rows(table, i):
            return table[bass.ds(i * NW, NW), :]

        def general_sp(sp):
            past = lambda s, value: wait_apart(sp, s, value, past_sp)
            sp.wait_ge(g_made, 5)
            for w in range(W):
                sp.dma_start(rows(xr_dram, w), XR[:, w, :]).then_inc(g_init, 16)
            for w in range(W + 1):
                sp.dma_start(rows(max_dram, w), g_fill[:, 0:H]).then_inc(g_init, 16)
                sp.dma_start(rows(acc_dram, w), g_fill[:, H:H + ZC]).then_inc(g_init, 16)
            sp.wait_ge(g_init, 16 * (3 * W + 2))
            with sp.Fori(0, GTILES) as i:
                sp.dma_start(g_edge, rows(edges, i)).then_inc(g_load[0][0], 16)
                sp.dma_start(g_src, src[bass.ds(i * NW, NW)].unsqueeze(1)).then_inc(g_load[0][1], 16)
                sp.dma_start(g_dst, dst[bass.ds(i * NW, NW)].unsqueeze(1)).then_inc(g_load[0][2], 16)
                past(g_dve[0], i * KD[0] + KD[0])
                sp.dma_start(rows(z_dram, i), g_z).then_inc(g_store[0], 16)
                sp.dma_start(rows(logit_dram, i), g_logit).then_inc(g_store[0], 16)
                past(g_store[0], i * 32 + 32)
                past(g_scat[0], i * 16 + 16)
            with sp.Fori(0, GTILES) as i:
                sp.dma_start(g_z, rows(z_dram, i)).then_inc(g_load[1][0], 16)
                sp.dma_start(g_logit, rows(logit_dram, i)).then_inc(g_load[1][1], 16)
                sp.dma_start(g_dst, dst[bass.ds(i * NW, NW)].unsqueeze(1)).then_inc(g_load[1][2], 16)
                past(g_scat[1], i * 16 + 16)
            with sp.Fori(0, W) as i:
                sp.dma_start(g_acc, rows(acc_dram, i)).then_inc(g_load[2][0], 16)
                sp.dma_start(g_x, rows(x, i)).then_inc(g_load[2][1], 16)
                sp.dma_start(g_xr, rows(xr_dram, i)).then_inc(g_load[2][2], 16)
                past(g_dve[2], i * KD[2] + KD[2])
                sp.dma_start(rows(out, i), y_out[:, 0, :]).then_inc(g_store[2], 16)
                past(g_store[2], i * 16 + 16)

        def general_pool(pool):
            past = lambda s, value: wait_apart(pool, s, value, past_pool)
            at_rows = lambda index: bass.IndirectOffsetOnAxis(ap=index, axis=0)
            nc.gpsimd.iota(g_iota[:, 0:1], pattern=[[0, 1]], base=NW, channel_multiplier=-1).then_inc(g_made, 1)
            nc.gpsimd.iota(g_iota[:, 1:2], pattern=[[0, 1]], base=N, channel_multiplier=1).then_inc(g_made, 1)
            nc.gpsimd.iota(g_down_i[:, :], pattern=[[-1, NW]], base=NW, channel_multiplier=0).then_inc(g_made, 1)
            pool.wait_ge(g_init, 16 * (3 * W + 2))
            with pool.Fori(0, GTILES) as i:
                for landed in g_load[0][1:]:
                    past(landed, i * 16 + 16)
                for k, (to, table, index) in enumerate(((g_xs, xs_dram, g_src), (g_xr, xr_dram, g_dst),
                                                        (g_max, max_dram, g_dst))):
                    nc.gpsimd.indirect_dma_start(to, None, table, at_rows(index)).then_inc(g_gath[0][k], 16)
                past(g_dve[0], i * KD[0] + KD[0])
                nc.gpsimd.indirect_dma_start(max_dram, at_rows(g_index[:, :]), g_newmax, None)\
                    .then_inc(g_scat[0], 16)
            with pool.Fori(0, GTILES) as i:
                past(g_load[1][2], i * 16 + 16)
                for k, (to, table) in enumerate(((g_max, max_dram), (g_acc, acc_dram))):
                    nc.gpsimd.indirect_dma_start(to, None, table, at_rows(g_dst)).then_inc(g_gath[1][k], 16)
                past(g_dve[1], i * KD[1] + KD[1])
                nc.gpsimd.indirect_dma_start(acc_dram, at_rows(g_index[:, :]), g_new, None)\
                    .then_inc(g_scat[1], 16)

        def general_pe(pe):
            unit = ident[0:NW, 0:NW]
            with pe.Fori(0, GTILES) as i:
                pe.wait_ge(g_load[0][0], i * 16 + 16)
                nc.tensor.transpose(p_edge, g_edge, unit).then_inc(g_pe[0], 1)
                pe.wait_ge(g_act[0], i * KA[0] + 1)
                nc.tensor.matmul(p_z, g_edgeT, we_sb[:, :], start=True, stop=True).then_inc(g_pe[0], 1)
                pe.wait_ge(g_dve[0], i * KD[0] + 11)
                nc.tensor.matmul(p_dst, g_dst_wide, unit, start=True, stop=True)
                for h in range(H):
                    last = nc.tensor.matmul(p_logit[:, h, :], g_logit_wide[:, h, :], unit, start=True, stop=True)
                last.then_inc(g_pe[0], 1)
            with pe.Fori(0, GTILES) as i:
                pe.wait_ge(g_dve[1], i * KD[1] + 2)
                nc.tensor.matmul(p_dst, g_dst_wide, unit, start=True, stop=True).then_inc(g_pe[1], 1)
                pe.wait_ge(g_dve[1], i * KD[1] + 13)
                nc.tensor.matmul(p_sum, g_same, g_msg, start=True, stop=True).then_inc(g_pe[1], 1)

        def general_act(act):
            with act.Fori(0, GTILES) as i:
                act.wait_ge(g_pe[0], i * KP[0] + 1)
                nc.scalar.copy(g_edgeT, p_edge).then_inc(g_act[0], 1)
                act.wait_ge(g_dve[0], i * KD[0] + 5)
                for k, (f, bias, scale) in enumerate(((ACT.Exp, 0.0, 1.0), (ACT.Square, c_one[0:NW, 0:1], 1.0),
                                                      (ACT.Ln, c_one[0:NW, 0:1], 1.0),
                                                      (ACT.Exp, c_ln2[0:NW, 0:1], -1.0))):
                    nc.scalar.activation(g_t, g_t, f, bias=bias, scale=scale).then_inc(g_act[0], 1)
                    act.wait_ge(g_act[0], i * KA[0] + 2 + k)
            with act.Fori(0, GTILES) as i:
                act.wait_ge(g_dve[1], i * KD[1] + 12)
                nc.scalar.activation(g_w, g_shift, ACT.Exp).then_inc(g_act[1], 1)
            with act.Fori(0, W) as i:
                act.wait_ge(g_dve[2], i * KD[2] + 9)
                nc.scalar.activation(lnv[:, :], mv[:, 1:2], ACT.Ln, bias=c_eps[0:NW, 0:1]).then_inc(g_act[2], 1)
                act.wait_ge(g_act[2], i * KA[2] + 1)
                nc.scalar.activation(rstd[:, :], lnv[:, :], ACT.Exp, scale=-0.5).then_inc(g_act[2], 1)

        def general_dve(dve):
            V = nc.vector

            def stepper(c, i):
                done = [0]

                def step(instruction):
                    instruction.then_inc(g_dve[c], 1)
                    done[0] += 1
                    if done[0] < KD[c]:
                        wait_apart(dve, g_dve[c], i * KD[c] + done[0], past_dve)
                    return done[0]
                return step

            def widen_receivers(step):
                step(V.tensor_copy(g_dstf, g_dst))
                step(V.tensor_copy(g_dst_wide, g_dstf.to_broadcast([NW, NW])))

            def find_same(step):
                step(V.tensor_scalar(g_same, p_dst, g_dstf, None, ALU.is_equal))
                step(V.tensor_tensor(g_rank, g_same, g_down, ALU.mult))
                step(V.tensor_reduce(g_lead, g_rank, AX.X, ALU.max))
                step(V.tensor_tensor(g_first, g_lead, g_self, ALU.is_equal))
                step(V.tensor_tensor(g_move, g_dstf, g_trash, ALU.subtract))
                step(V.tensor_tensor(g_moved, g_move, g_first, ALU.mult))
                step(V.tensor_tensor(g_index[:, :], g_moved, g_trash, ALU.add))

            heads = lambda ap: ap.rearrange("p (h d) -> p h d", h=H)
            wide = lambda ap: ap.unsqueeze(2).to_broadcast([NW, H, HD])
            V.memset(g_fill[:, 0:H], -FAR).then_inc(g_made, 1)
            V.memset(g_fill[:, H:H + ZC], 0.0).then_inc(g_made, 1)
            dve.wait_ge(g_made, 5)
            V.tensor_copy(g_self, g_iota[:, 0:1]).then_inc(g_made, 1)
            V.tensor_copy(g_trash, g_iota[:, 1:2]).then_inc(g_made, 1)
            V.tensor_copy(g_down, g_down_i[:, :]).then_inc(g_made, 1)
            dve.wait_ge(g_made, 8)
            with dve.Fori(0, GTILES) as i:
                step = stepper(0, i)
                for landed in g_load[0]:
                    dve.wait_ge(landed, i * 16 + 16)
                widen_receivers(step)
                for landed in g_gath[0]:
                    dve.wait_ge(landed, i * 16 + 16)
                dve.wait_ge(g_pe[0], i * KP[0] + 2)
                step(V.tensor_tensor(g_z, p_z, g_xs, ALU.add))
                step(V.tensor_tensor(g_z, g_z, g_xr, ALU.add))
                step(V.tensor_scalar(g_t, g_z, ZMAX, None, ALU.min))
                dve.wait_ge(g_act[0], i * KA[0] + KA[0])
                step(V.scalar_tensor_tensor(out=g_t, in0=g_t, scalar=1.0, in1=g_z, op0=ALU.subtract,
                                            op1=ALU.mult, reverse0=True))
                step(V.tensor_tensor(g_t, g_t, attn_row[0:NW, :, :].rearrange("p h d -> p (h d)"), ALU.mult))
                step(V.tensor_reduce(g_logit, heads(g_t), AX.X, ALU.add))
                step(V.tensor_scalar(g_logit, g_logit, attn_bias[0:NW, 0:1], None, ALU.add))
                step(V.tensor_copy(g_logit_wide, g_logit.unsqueeze(2).to_broadcast([NW, H, NW])))
                step(V.tensor_copy(g_newmax, g_max))
                dve.wait_ge(g_pe[0], i * KP[0] + 3)
                find_same(step)
                step(V.tensor_scalar(g_bar, g_same, 1.0, FAR, ALU.subtract, ALU.mult))
                step(V.tensor_tensor(g_barred, p_logit, g_bar.unsqueeze(1).to_broadcast([NW, H, NW]), ALU.add))
                V.tensor_reduce(g_tmax, g_barred, AX.X, ALU.max).then_inc(past_max, 1)
                wait_apart(dve, past_max, i + 1, past_dve)
                step(V.tensor_tensor(g_newmax, g_newmax, g_tmax, ALU.max))
            with dve.Fori(0, GTILES) as i:
                step = stepper(1, i)
                for landed in g_load[1]:
                    dve.wait_ge(landed, i * 16 + 16)
                widen_receivers(step)
                dve.wait_ge(g_pe[1], i * KP[1] + 1)
                find_same(step)
                for landed in g_gath[1]:
                    dve.wait_ge(landed, i * 16 + 16)
                step(V.tensor_copy(g_newmax, g_max))
                step(V.tensor_copy(g_new, g_acc))
                step(V.tensor_tensor(g_shift, g_logit, g_newmax, ALU.subtract))
                dve.wait_ge(g_act[1], i * KA[1] + 1)
                V.tensor_copy(g_msg[:, D:ZC], g_w).then_inc(past_w, 1)
                wait_apart(dve, past_w, i + 1, past_dve)
                step(V.tensor_tensor(heads(g_msg[:, 0:D]), heads(g_z), wide(g_w), ALU.mult))
                dve.wait_ge(g_pe[1], i * KP[1] + 2)
                step(V.tensor_tensor(g_new, g_new, p_sum, ALU.add))
            with dve.Fori(0, W) as i:
                step = stepper(2, i)
                for landed in g_load[2]:
                    dve.wait_ge(landed, i * 16 + 16)
                step(V.tensor_scalar(den[:, :], g_acc[:, D:ZC], TINY, None, ALU.max))
                step(V.tensor_scalar(has[:, :], g_acc[:, D:ZC], 0.0, None, ALU.is_gt))
                step(V.reciprocal(rden[:, :], den[:, :]))
                step(V.tensor_tensor(heads(att[:, :]), heads(g_acc[:, 0:D]), wide(rden[:, :]), ALU.mult))
                step(V.tensor_tensor(heads(rcv[:, :]), heads(g_xr), wide(has[:, :]), ALU.mult))
                step(V.tensor_tensor(att2[:, :], att[:, :], rcv[:, :], ALU.subtract))
                step(V.tensor_tensor(y[:, :], att2[:, :], g_x, ALU.add))
                step(V.bn_stats(stats[:, :], y[:, :]))
                step(V.bn_aggr(mv[:, :], stats[:, :]))
                dve.wait_ge(g_act[2], i * KA[2] + 2)
                step(V.tensor_scalar(y_out[:, 0, :], y[:, :], mv[:, 0:1], rstd[:, 0:1], ALU.subtract, ALU.mult))

        block = ctx.enter_context(nc.Block())

        @block.sync
        def _(sp):
            def load_edges(b, start):
                sp.dma_start(edge_buf[:, b, :, :],
                             edges[bass.ds(start, CAP), :].rearrange("(p t) d -> p t d", t=T))\
                    .then_inc(edge_landed[b], 16)

            def load_indices(b, start):
                sp.dma_start(src_i[:, b, :], src[bass.ds(start, CAP)].rearrange("(p t) -> p t", t=T))\
                    .then_inc(src_landed[b], 16)
                sp.dma_start(dst_i[:, b, :], dst[bass.ds(start, CAP)].rearrange("(p t) -> p t", t=T))\
                    .then_inc(dst_landed[b], 16)

            def load_x(w, b):
                sp.dma_start(x_in[:, b, :], x[bass.ds(w * NW, NW), :]).then_inc(x_landed[b], 16)

            def store(w, b):
                wait_apart(sp, fin, w * FIN + FIN, past_sp)
                sp.dma_start(out[bass.ds(w * NW, NW), :], y_out[:, b, :]).then_inc(stored[b], 16)

            def load(w, b):
                start = sp.value_load(start_i[0:1, bass.ds(w, 1)], min_val=0, max_val=E - CAP)
                wait_apart(sp, edgeT_ps, at(w - 2, NG - 1), past_sp)
                load_edges(b, start)
                wait_apart(sp, z_ready, at(w - 2, NG - 1), past_sp)
                wait_apart(sp, prep, (w - 1) * PREP, past_sp)
                load_indices(b, start)

            for b in range(2):
                sp.sem_inc(stored[b], 1)
            sp.dma_start(wsr_sb[:, 0, :], ws_k.rearrange("f h d -> f (h d)")).then_inc(s_const, 16)
            sp.dma_start(wsr_sb[:, 1, :], wr_k.rearrange("f h d -> f (h d)")).then_inc(s_const, 16)
            for k, bias in enumerate((ws_b, we_b, wr_b)):
                sp.dma_start(bias_in[:, k, :], bias.rearrange("(o h) d -> o (h d)", o=1).to_broadcast([NW, D]))\
                    .then_inc(s_const, 16)
            by_part = dst.rearrange("(p j) -> p j", j=EP)
            sp.dma_start(dst_all, by_part).then_inc(s_dall, 16)
            sp.dma_start(next_first[0:NW - 1, :], by_part[1:NW, 0:1], allow_slow_non_contiguous=True)\
                .then_inc(s_dall, 16)
            sp.dma_start(next_first[NW - 1:NW, :], by_part[NW - 1:NW, EP - 1:EP], allow_slow_non_contiguous=True)\
                .then_inc(s_dall, 16)
            xw = x.rearrange("(w p) d -> p w d", p=NW)
            for c in range(XPARTS):
                for lo, hi in ROW_PARTS:
                    sp.dma_start(x_all[lo:hi, c * XN:(c + 1) * XN, :], xw[lo:hi, c * XN:(c + 1) * XN, :])\
                        .then_inc(s_xall[c], 16)
            sp.dma_start(we_sb[:, :], we_k.rearrange("f h d -> f (h d)")).then_inc(s_later, 16)
            for h in range(H):
                sp.dma_start(attn_row[:, h, :], attn_w.rearrange("d o -> o d").to_broadcast([P, HD]))\
                    .then_inc(s_later, 16)
            sp.wait_ge(s_vconst, 1)
            for h in range(H):
                sp.dma_start(attn_cols[h * HD:(h + 1) * HD, h:h + 1], attn_w).then_inc(s_later, 16)
            sp.dma_start(attn_bias[:, :], attn_b.rearrange("(a b) -> a b", a=1).to_broadcast([P, 1]))\
                .then_inc(s_later, 16)
            load_indices(0, 0)
            load_edges(0, 0)
            load_x(0, 0)
            load_x(1, 1)
            tw = xs_dram.rearrange("(w p) d -> p w d", p=NW)
            for c in range(XPARTS):
                sp.wait_ge(s_xsr, 2 * XN * (c + 1))
                for lo, hi in ROW_PARTS:
                    sp.dma_start(tw[lo:hi, c * XN:(c + 1) * XN, :], xs_stage[lo:hi, c * XN:(c + 1) * XN, :])\
                        .then_inc(s_table, 16)
            sp.wait_ge(s_start, 1)
            start = sp.value_load(start_i[0:1, 1:2], min_val=0, max_val=E - CAP)
            load_edges(1, start)
            load_indices(1, start)
            load(2, 0)
            load(3, 1)
            store(0, 0)
            load_x(2, 0)
            with sp.Fori(2, W // 2) as i:
                load(i * 2, 0)
                store(i * 2 - 3, 1)
                load_x(i * 2 - 1, 1)
                load(i * 2 + 1, 1)
                store(i * 2 - 2, 0)
                load_x(i * 2, 0)
            store(W - 3, 1)
            load_x(W - 1, 1)
            store(W - 2, 0)
            store(W - 1, 1)
            for b in range(2):
                sp.wait_ge(stored[b], 16 * (W // 2) + 1)
            sp.sem_inc(s_sorted_done, 1)
            general(sp, general_sp)

        @block.gpsimd
        def _(pool):
            nc.gpsimd.memset(ident[:, :], 0.0).then_inc(s_pool, 1)
            pool.wait_ge(s_pool, 1)
            nc.gpsimd.affine_select(out=ident[:, :], in_=ident[:, :], compare_op=ALU.not_equal, fill=1.0,
                                    base=0, pattern=[[-1, P]], channel_multiplier=1).then_inc(s_pool, 1)
            nc.gpsimd.iota(iota_i[:, :], pattern=[[1, NW]], base=0, channel_multiplier=0).then_inc(s_pool, 1)
            nc.gpsimd.iota(bound_i[:, :], pattern=[[NW, W]], base=0, channel_multiplier=0).then_inc(s_pool, 1)

            def gathers(b):
                for g, (a, n) in enumerate(GROUPS):
                    for t in range(a, a + n):
                        nc.gpsimd.indirect_dma_start(
                            gath[:, b, t, :], None, xs_dram,
                            bass.IndirectOffsetOnAxis(ap=src_i[:, b, t:t + 1], axis=0))\
                            .then_inc(gath_landed[b][g], 16)

            pool.wait_ge(s_table, 16 * 2 * XPARTS)
            pool.wait_ge(src_landed[0], 16)
            gathers(0)
            pool.wait_ge(s_search, SEARCH)
            pool.wait_ge(src_landed[1], 16)
            gathers(1)
            with pool.Fori(1, W // 2) as i:
                for b in range(2):
                    pool.wait_ge(src_landed[b], i * 16 + 16)
                    wait_apart(pool, z_ready, at(i * 2 + b - 2, NG - 1), past_pool)
                    gathers(b)
            general(pool, general_pool)

        @block.tensor
        def _(pe):
            def turn_x(w):
                pe.wait_ge(s_xall[w // XN], 32)
                wait(pe, s_xT, w - 1)
                nc.tensor.transpose(ps_edgeT[w % 2][:, 0, 0:NW], x_all[:, w, :], ident[0:NW, 0:NW])\
                    .then_inc(s_xT_ps, 1)

            pe.wait_ge(s_pool, 2)
            pe.wait_ge(s_const, 16 * NCONST)
            turn_x(0)
            for w in range(W):
                if w + 1 < W:
                    turn_x(w + 1)
                pe.wait_ge(s_xT, w + 1)
                wait(pe, s_xsr, 2 * (w - 1))
                nc.tensor.matmul(ps_onehotT[w % 2][0:NW, 0:2, :], xT[:, w % 2, :], wsr_sb[:, :, :],
                                 start=True, stop=True).then_inc(s_xsr_ps, 1)
            pe.wait_ge(s_later, 16 * NLATER)
            pe.wait_ge(s_search, SEARCH)
            nc.tensor.matmul(ps_ends[0:1, 0:W + 2], ones[0:NW, 0:1], counts[:, :], start=True, stop=True)\
                .then_inc(s_count, 1)

            def turn(w, b, k, g):
                a, n = GROUPS[g]
                q = (b + g) % 2
                if g == 0:
                    pe.wait_ge(edge_landed[b], k * 16 + 16)
                wait(pe, edgeT_ready, at(w, g) - 2)
                for j in range(n):
                    tr = nc.tensor.transpose(ps_edgeT[q][:, j, :], edge_buf[:, b, a + j, :], ident[:, :])
                tr.then_inc(edgeT_ps, 1)
                pe.wait_ge(onehot_ready, at(w, g))
                wait(pe, onehotT_ready, at(w, g) - 2)
                for j in range(n):
                    tr = nc.tensor.transpose(ps_onehotT[q][0:NW, j, :].bitcast(BF16)[:, 0:P],
                                             halves(OHv[:, b, a + j, :]), ident_half[:, :])
                tr.then_inc(onehotT_ps, 1)

            def products(w, b, g):
                a, n = GROUPS[g]
                q = (b + g) % 2
                pe.wait_ge(edgeT_ready, at(w, g))
                pe.wait_ge(onehotT_ready, at(w, g))
                wait(pe, z_ready, at(w, g) - 2)
                for j in range(n):
                    nc.tensor.matmul(ps_z[q][:, j, :], edgeT[:, q, j, :], we_sb[:, :], start=True, stop=False)
                    mm = nc.tensor.matmul(ps_z[q][:, j, :], onehotT[:, q, j, :], XR[:, bass.ds(w, 1), :],
                                          start=False, stop=True)
                mm.then_inc(z_ps, 1)

            def turn_mish(w, g):
                if g == TURNED[0]:
                    if there(w - 1):
                        wait_apart(pe, seg, (w - 1) * SEG + SEG_A + SEG_B + ENDS_READ, past_pe)
                else:
                    pe.wait_ge(mishT_ready, at_turned(w, g) - 1)
                pe.wait_ge(mish_ready, at(w, g))
                for j in range(TURN_T):
                    tr = nc.tensor.transpose(ps_mishT[:, j, :], tbuf[:, g % NT, j * D:(j + 1) * D], ident[:, :])
                tr.then_inc(mishT_ps, 1)

            def sum_heads(w, g):
                pe.wait_ge(mishT_ready, at_turned(w, g))
                for j in range(TURN_T):
                    c = (TURNED.index(g) * TURN_T + j) * H
                    mm = nc.tensor.matmul(ps_logit[:, c:c + H], mishT[:, j, :], attn_cols[:, :],
                                          start=True, stop=True)
                mm.then_inc(heads_ps, 1)

            def sums(w, b, g):
                a, n = GROUPS[g]
                if g == 0:
                    wait(pe, fin, (w - 1) * FIN + FIN_READ)
                pe.wait_ge(msg_ready, at(w, g))
                for t in range(a, a + n):
                    mm = nc.tensor.matmul(ps_sum[0:NW, 0:ZC], OHv[:, b, t, :], Zv[:, b, t, :],
                                          start=(t == 0), stop=(t == T - 1))
                mm.then_inc(sum_ready, 1)

            def ends_to_row(w, b):
                pe.wait_ge(seg, w * SEG + SEG_A)
                for c, ends in enumerate((row_max[:, :, 0], row_max[:, :, T - 1],
                                          far_ends[:, b, 0, :], far_ends[:, b, 1, :])):
                    tr = nc.tensor.transpose(ps_ends[0:H, c * P:(c + 1) * P], ends, ident[:, :])
                tr.then_inc(ends_ps, 1)

            def maxima_back(w):
                wait_apart(pe, seg, w * SEG + SEG_A + SEG_B, past_pe)
                im = item_max[:, :].rearrange("h (p k) -> h k p", k=2)
                for c in range(2):
                    tr = nc.tensor.transpose(ps_ends[:, c * H:(c + 1) * H], im[:, c, :], ident[0:H, 0:H])
                tr.then_inc(back_ps, 1)

            def window(w, b, k):
                for g in range(NG):
                    if there(w):
                        products(w, b, g)
                    w1, b1, g1 = after(w, b, g)
                    if there(w1) and there(w):
                        turn(w1, b1, k if w1 is w else (k + b if b else k), g1)
                    for m in SUM_LAST.get(g, []) if there(w - 2) else []:
                        sums(w - 2, b, m)
                    if g == 1 and there(w - 1):
                        ends_to_row(w - 1, 1 - b)
                    if g == 3 and there(w - 1):
                        maxima_back(w - 1)
                    for m in SUM_NEXT.get(g, []) if there(w - 1) else []:
                        sums(w - 1, 1 - b, m)
                    w3, _, g3 = back(w, b, g, 3)
                    if g3 in TURNED and there(w3):
                        sum_heads(w3, g3)
                    w2, _, g2 = back(w, b, g, 2)
                    if g2 in TURNED and there(w2):
                        turn_mish(w2, g2)

            turn(0, 0, 0, 0)
            run(pe, window)
            general(pe, general_pe)

        @block.scalar
        def _(act):
            nc.scalar.preload_act_table_set("natural_log_exp_and_others")
            for w in range(W):
                act.wait_ge(s_xT_ps, w + 1)
                wait(act, s_xsr_ps, w - 1)
                nc.scalar.copy(xT[:, w % 2, :], ps_edgeT[w % 2][:, 0, 0:NW]).then_inc(s_xT, 1)
            act.wait_ge(s_vconst, VCONST)

            def copy_edgeT(w, b, g):
                n = GROUPS[g][1]
                q = (b + g) % 2
                act.wait_ge(edgeT_ps, at(w, g))
                wait(act, z_ps, at(w, g) - 2)
                nc.scalar.copy(edgeT[:, q, 0:n, :], ps_edgeT[q][:, 0:n, :]).then_inc(edgeT_ready, 1)

            def copy_onehotT(w, b, g):
                n = GROUPS[g][1]
                q = (b + g) % 2
                act.wait_ge(onehotT_ps, at(w, g))
                wait(act, z_ps, at(w, g) - 2)
                nc.scalar.copy(onehotT[:, q, 0:n, :], ps_onehotT[q][0:NW, 0:n, :].bitcast(BF16)[:, :, 0:P])\
                    .then_inc(onehotT_ready, 1)

            def copy_mishT(w, g):
                act.wait_ge(mishT_ps, at_turned(w, g))
                wait(act, heads_ps, at_turned(w, g) - 1)
                nc.scalar.copy(mishT[:, :, :], ps_mishT[:, 0:TURN_T, :]).then_inc(mishT_ready, 1)

            def ratio_step(w, g, k):
                tb = tbuf[:, g % NT, 0:GROUPS[g][1] * D]
                if k == 0:
                    act.wait_ge(clamped, at(w, g))
                    nc.scalar.activation(tb, tb, ACT.Exp).then_inc(exp_done, 1)
                elif k == 1:
                    act.wait_ge(exp_done, at(w, g))
                    nc.scalar.activation(tb, tb, ACT.Square, bias=c_one[:, 0:1]).then_inc(sq_done, 1)
                elif k == 2:
                    act.wait_ge(sq_done, at(w, g))
                    nc.scalar.activation(tb, tb, ACT.Ln, bias=c_one[:, 0:1]).then_inc(ln_done, 1)
                else:
                    act.wait_ge(ln_done, at(w, g))
                    nc.scalar.activation(tb, tb, ACT.Exp, bias=c_ln2[:, 0:1], scale=-1.0).then_inc(ratio_ready, 1)

            def items(w):
                act.wait_ge(ends_ps, w + 1)
                nc.scalar.copy(item_val[:, :, :].rearrange("h p k -> h k p"),
                               ps_ends[0:H, 0:2 * P].rearrange("h (k p) -> h k p", k=2)).then_inc(items_ready, 1)
                nc.scalar.copy(item_far[:, :, :].rearrange("h p k -> h k p"),
                               ps_ends[0:H, 2 * P:4 * P].rearrange("h (k p) -> h k p", k=2))\
                    .then_inc(items_ready, 1)

            def weights(w, b):
                act.wait_ge(seg, w * SEG + SEG)
                nc.scalar.activation(Zv[:, b, :, D:ZC].rearrange("p t h -> p h t"), shifted[:, :, :], ACT.Exp)\
                    .then_inc(w_ready, 1)

            def inverse_std(w):
                act.wait_ge(fin, w * FIN + FA)
                nc.scalar.activation(lnv[:, :], mv[:, 1:2], ACT.Ln, bias=c_eps[0:NW, 0:1]).then_inc(rstd_step, 1)
                act.wait_ge(rstd_step, w * 2 + 1)
                nc.scalar.activation(rstd[:, :], lnv[:, :], ACT.Exp, scale=-0.5).then_inc(rstd_step, 1)

            def window(w, b, k):
                for g in range(NG):
                    w1, b1, g1 = after(w, b, g)
                    w2, _, g2 = back(w, b, g, 2)
                    here, coming = there(w), there(w1) and there(w)
                    if coming:
                        copy_edgeT(w1, b1, g1)
                        copy_onehotT(w1, b1, g1)
                    if here:
                        ratio_step(w, g, 0)
                        ratio_step(w, g, 1)
                    if here:
                        ratio_step(w, g, 2)
                    if g2 in TURNED and there(w2):
                        copy_mishT(w2, g2)
                    if g == 1 and there(w - 1):
                        items(w - 1)
                    if here:
                        ratio_step(w, g, 3)
                    if g == 6 and there(w - 2):
                        inverse_std(w - 2)
                    if g == 3 and there(w - 1):
                        weights(w - 1, 1 - b)

            copy_edgeT(0, 0, 0)
            copy_onehotT(0, 0, 0)
            run(act, window)
            general(act, general_act)

        @block.vector
        def _(dve):
            nc.vector.memset(attn_cols[:, :], 0.0).then_inc(s_vconst, 1)
            nc.vector.memset(c_one[:, :], 1.0).then_inc(s_vconst, 1)
            nc.vector.memset(c_ln2[:, :], LN2).then_inc(s_vconst, 1)
            nc.vector.memset(c_eps[:, :], EPS).then_inc(s_vconst, 1)
            nc.vector.memset(ones[:, :], 1.0).then_inc(s_vconst, 1)
            nc.vector.memset(pen[:, :, :], -FAR).then_inc(s_vconst, 1)
            nc.vector.memset(item_pen[:, :], -FAR).then_inc(s_vconst, 1)
            nc.vector.memset(window_base[:, :], -float(NW)).then_inc(s_vconst, 1)
            dve.wait_ge(s_pool, 4)
            nc.vector.tensor_copy(iota_f[:, :], iota_i[:, :]).then_inc(s_vconst, 1)
            nc.vector.tensor_copy(bound[:, :], bound_i[:, :]).then_inc(s_vconst, 1)
            nc.vector.tensor_copy(ident_half[:, :], ident[:, :]).then_inc(s_vconst, 1)
            dve.wait_ge(s_vconst, BOUNDS)
            dve.wait_ge(s_dall, 48)
            seen = dst_all.rearrange("p (s k) -> p s k", k=STEP)[:, :, 0]
            nc.vector.tensor_tensor(below, seen.unsqueeze(1).to_broadcast([NW, W, NS]),
                                    bound[:, :].unsqueeze(2).to_broadcast([NW, W, NS]), ALU.is_lt)\
                .then_inc(s_search, 1)
            dve.wait_ge(s_search, 1)
            nc.vector.tensor_reduce(counts[:, 0:W], below, AX.X, ALU.add).then_inc(s_search, 1)
            dve.wait_ge(s_const, 16 * NCONST)
            nc.vector.tensor_tensor(bias_sr[:, 0, :], bias_in[:, 0, :], bias_in[:, 1, :], ALU.add)\
                .then_inc(s_vconst, 1)
            nc.vector.tensor_copy(bias_sr[:, 1, :], bias_in[:, 2, :]).then_inc(s_vconst, 1)
            dve.wait_ge(s_vconst, VCONST)
            for w in range(W):
                dve.wait_ge(s_xsr_ps, w + 1)
                nc.vector.tensor_tensor(xs_stage[:, w, :], ps_onehotT[w % 2][0:NW, 0, :], bias_sr[:, 0, :],
                                        ALU.add).then_inc(s_xsr, 1)
                nc.vector.tensor_tensor(XR[:, w, :], ps_onehotT[w % 2][0:NW, 1, :], bias_sr[:, 1, :],
                                        ALU.add).then_inc(s_xsr, 1)

            dve.wait_ge(s_later, 16 * NLATER)
            dve.wait_ge(s_search, 2)
            fall = gath[0:NW, 1, :, :].rearrange("p t d -> p (t d)")[:, 0:EP - 1]
            nc.vector.tensor_tensor(fall, dst_all[:, 1:EP], dst_all[:, 0:EP - 1], ALU.is_lt).then_inc(s_search, 1)
            nc.vector.tensor_tensor(counts[0:NW, W + 1:W + 2], next_first[:, :], dst_all[:, EP - 1:EP], ALU.is_lt)\
                .then_inc(s_search, 1)
            dve.wait_ge(s_search, 4)
            nc.vector.tensor_reduce(counts[:, W:W + 1], fall, AX.X, ALU.add).then_inc(s_search, 1)
            dve.wait_ge(s_count, 1)
            nc.vector.tensor_scalar(start_f[:, :], ps_ends[0:1, 0:W], float(STEP), -float(STEP), ALU.mult,
                                    ALU.add).then_inc(s_search, 1)
            dve.wait_ge(s_search, SEARCH + 1)
            nc.vector.tensor_scalar(start_i[:, :], start_f[:, :], 0.0, float(E - CAP), ALU.max, ALU.min)\
                .then_inc(s_start, 1)
            nc.vector.tensor_scalar(start_c[:, :], start_f[:, :], 0.0, float(E - CAP), ALU.max, ALU.min)\
                .then_inc(s_flag, 1)
            nc.vector.memset(run_end[:, W - 1:W], float(E)).then_inc(s_flag, 1)
            nc.vector.tensor_scalar(run_end[:, 0:W - 1], ps_ends[0:1, 1:W], float(STEP), None, ALU.mult)\
                .then_inc(s_flag, 1)
            nc.vector.tensor_copy(late[:, W:W + 2], ps_ends[0:1, W:W + 2]).then_inc(s_flag, 1)
            dve.wait_ge(s_flag, 4)
            nc.vector.scalar_tensor_tensor(out=late[:, 0:W], in0=start_c[:, :], scalar=float(CAP),
                                           in1=run_end[:, :], op0=ALU.add, op1=ALU.is_lt).then_inc(s_flag, 1)
            dve.wait_ge(s_flag, 5)
            nc.vector.tensor_reduce(flag_f[:, :], late[:, :], AX.X, ALU.add).then_inc(s_flag, 1)
            dve.wait_ge(s_flag, 6)
            nc.vector.tensor_copy(flag_i[:, :], flag_f[:, :]).then_inc(s_flag, 1)

            def prepare(w, b, k, part):
                base = w * PREP
                if part == 0:
                    nc.vector.tensor_scalar(window_base[:, :], window_base[:, :], float(NW), None, ALU.add)\
                        .then_inc(prep, 1)
                elif part == 1:
                    dve.wait_ge(dst_landed[b], k * 16 + 16)
                    dve.wait_ge(prep, base + 1)
                    nc.vector.tensor_scalar(local[:, b, :], dst_i[:, b, :], window_base[:, 0:1], None, ALU.subtract)\
                        .then_inc(prep, 1)
                    nc.vector.tensor_scalar(far[:, b, :], dst_i[:, b, :], FAR, None, ALU.mult).then_inc(prep, 1)
                elif part == 2:
                    dve.wait_ge(prep, base + 3)
                    f = far[:, b, :].unsqueeze(1)
                    nc.vector.tensor_tensor(pen[:, b, 0:H * T].rearrange("p (h t) -> p h t", t=T)[:, :, 1:T],
                                            f[:, :, 0:T - 1].to_broadcast([P, H, T - 1]),
                                            f[:, :, 1:T].to_broadcast([P, H, T - 1]), ALU.subtract).then_inc(prep, 1)
                    nc.vector.tensor_scalar(pen_head[:, b, :], far[:, b, :], far[:, b, 0:1], -1.0, ALU.subtract,
                                            ALU.mult).then_inc(prep, 1)
                    nc.vector.tensor_scalar(pen_tail[:, b, :], far[:, b, :], far[:, b, T - 1:T], None,
                                            ALU.subtract).then_inc(prep, 1)
                    nc.vector.tensor_copy(far_ends[:, b, :, :],
                                          far[:, b, 0:T:T - 1].unsqueeze(2).to_broadcast([P, 2, H])).then_inc(prep, 1)

            def one_hots(w, b, g):
                a, n = GROUPS[g]
                wait(dve, sum_ready, at(w - 2, g))
                dve.wait_ge(prep, w * PREP + 2)
                nc.vector.tensor_tensor(OHv[:, b, a:a + n, :],
                                        iota_f[:, :].unsqueeze(1).to_broadcast([P, n, NW]),
                                        local[:, b, a:a + n].unsqueeze(2).to_broadcast([P, n, NW]),
                                        ALU.is_equal).then_inc(onehot_ready, 1)

            def add_gathered(w, b, k, g):
                a, n = GROUPS[g]
                dve.wait_ge(z_ps, at(w, g))
                dve.wait_ge(gath_landed[b][g], k * (16 * n) + 16 * n)
                nc.vector.tensor_tensor(Zv[:, b, a:a + n, 0:D], ps_z[(b + g) % 2][:, 0:n, :],
                                        gath[:, b, a:a + n, :], ALU.add).then_inc(z_ready, 1)

            def clamp(w, b, g):
                a, n = GROUPS[g]
                dve.wait_ge(z_ready, at(w, g))
                wt, _, gt = back(w, b, g, NT)
                if gt in TURNED and there(wt):
                    dve.wait_ge(mishT_ps, at_turned(wt, gt))
                tb = tbuf[:, g % NT, 0:n * D].rearrange("p (t d) -> p t d", d=D)
                nc.vector.tensor_scalar(tb, Zv[:, b, a:a + n, 0:D], ZMAX, None, ALU.min).then_inc(clamped, 1)

            def mish(w, b, g):
                a, n = GROUPS[g]
                dve.wait_ge(ratio_ready, at(w, g))
                tb = tbuf[:, g % NT, 0:n * D].rearrange("p (t d) -> p t d", d=D)
                nc.vector.scalar_tensor_tensor(out=tb, in0=tb, scalar=1.0, in1=Zv[:, b, a:a + n, 0:D],
                                               op0=ALU.subtract, op1=ALU.mult, reverse0=True)\
                    .then_inc(mish_ready, 1)

            def read_heads(w, b):
                a = GROUPS[TURNED[0]][0]
                turned = logit[:, b, :, a:a + len(TURNED) * GT].rearrange("p h (g t) -> p g t h", t=GT)
                dve.wait_ge(heads_ps, at_turned(w, TURNED[-1]))
                nc.vector.tensor_copy(turned[:, :, 0:TURN_T, :],
                                      ps_logit.rearrange("p (g t h) -> p g t h", h=H, t=TURN_T))\
                    .then_inc(heads_read, 1)

            def first_tile(g):
                return TURN_T if g in TURNED else 0

            def score(w, b, g):
                lo, n = first_tile(g), GROUPS[g][1]
                dve.wait_ge(mish_ready, at(w, g))
                tb = tbuf[:, g % NT, lo * D:n * D].rearrange("p (t d) -> p t d", d=D)
                row = attn_row[:, :, :].rearrange("p h d -> p (h d)").unsqueeze(1)
                nc.vector.tensor_tensor(tb, tb, row.to_broadcast([P, n - lo, D]), ALU.mult).then_inc(scored, 1)

            def reduce_heads(w, b, g):
                a, n = GROUPS[g]
                lo = first_tile(g)
                dve.wait_ge(scored, at(w, g))
                tb = tbuf[:, g % NT, lo * D:n * D].rearrange("p (t h d) -> p t h d", h=H, d=HD)
                nc.vector.tensor_reduce(logit[:, b, :, a + lo:a + n].rearrange("p h t -> p t h"), tb, AX.X, ALU.add)\
                    .then_inc(logit_ready, 1)

            def maxima_in_partitions(w, b):
                base = w * SEG
                lg = logit[:, b, :, :].rearrange("p h t -> p (h t)")
                run_ = run_max[:, :, :].rearrange("p h t -> p (h t)")
                row_ = row_max[:, :, :].rearrange("p h t -> p (h t)")
                dve.wait_ge(logit_ready, at(w, NG - 1))
                dve.wait_ge(heads_read, w + 1)
                nc.vector.tensor_scalar(lg, lg, attn_bias[:, 0:1], None, ALU.add).then_inc(seg, 1)
                dve.wait_ge(seg, base + 1)
                nc.vector.tensor_tensor_scan(run_, pen[:, b, 0:H * T], lg, 0.0, ALU.add, ALU.max).then_inc(seg, 1)
                dve.wait_ge(seg, base + 2)
                nc.vector.tensor_tensor_scan(row_[:, ::-1], pen[:, b, 1:H * T + 1][:, ::-1], run_[:, ::-1], 0.0,
                                             ALU.add, ALU.max).then_inc(seg, 1)

            def maxima_over_partitions(w):
                base = w * SEG + SEG_A
                dve.wait_ge(items_ready, w * 2 + 2)
                far_ = item_far[:, :, :].rearrange("h p k -> h (p k)")
                val_ = item_val[:, :, :].rearrange("h p k -> h (p k)")
                nc.vector.tensor_tensor(item_pen[:, 1:2 * P], far_[:, 0:2 * P - 1], far_[:, 1:2 * P],
                                        ALU.subtract).then_inc(seg, 1)
                dve.wait_ge(seg, base + 1)
                nc.vector.tensor_tensor_scan(item_run[:, :], item_pen[:, 0:2 * P], val_, 0.0, ALU.add, ALU.max)\
                    .then_inc(seg, 1)
                dve.wait_ge(seg, base + 2)
                nc.vector.tensor_tensor_scan(item_max[:, ::-1], item_pen[:, 1:2 * P + 1][:, ::-1],
                                             item_run[:, ::-1], 0.0, ALU.add, ALU.max).then_inc(seg, 1)

            def subtract_maxima(w, b, part):
                base = w * SEG + SEG_A + SEG_B
                if part == 0:
                    dve.wait_ge(back_ps, w + 1)
                    for k, pens in enumerate((pen_head, pen_tail)):
                        nc.vector.tensor_tensor(ends_max[:, k, :, :],
                                                pens[:, b, :].unsqueeze(1).to_broadcast([P, H, T]),
                                                ps_ends[:, k * H:(k + 1) * H].unsqueeze(2).to_broadcast([P, H, T]),
                                                ALU.add).then_inc(seg, 1)
                elif part == 1:
                    dve.wait_ge(seg, base + 2)
                    nc.vector.tensor_tensor(seg_max[:, :, :], ends_max[:, 0, :, :], ends_max[:, 1, :, :], ALU.max)\
                        .then_inc(seg, 1)
                elif part == 2:
                    dve.wait_ge(seg, base + 3)
                    nc.vector.tensor_tensor(seg_max[:, :, :], seg_max[:, :, :], row_max[:, :, :], ALU.max)\
                        .then_inc(seg, 1)
                elif part == 3:
                    dve.wait_ge(seg, base + 4)
                    nc.vector.tensor_tensor(shifted[:, :, :], logit[:, b, :, :], seg_max[:, :, :], ALU.subtract)\
                        .then_inc(seg, 1)

            def messages(w, b, g):
                a, n = GROUPS[g]
                dve.wait_ge(w_ready, w + 1)
                zz = Zv[:, b, a:a + n, 0:D].rearrange("p t (h d) -> p t h d", h=H)
                ww = Zv[:, b, a:a + n, D:ZC].unsqueeze(3).to_broadcast([P, n, H, HD])
                nc.vector.tensor_tensor(zz, zz, ww, ALU.mult).then_inc(msg_ready, 1)

            def attended(w, part):
                base = w * FIN
                heads = lambda ap: ap.rearrange("p (h d) -> p h d", h=H)
                wide = lambda ap: ap.unsqueeze(2).to_broadcast([NW, H, HD])
                if part == 0:
                    dve.wait_ge(sum_ready, at(w, NG - 1))
                    nc.vector.tensor_scalar(den[:, :], ps_sum[0:NW, D:ZC], TINY, None, ALU.max).then_inc(fin, 1)
                    nc.vector.tensor_scalar(has[:, :], ps_sum[0:NW, D:ZC], 0.0, None, ALU.is_gt).then_inc(fin, 1)
                elif part == 1:
                    dve.wait_ge(fin, base + 2)
                    nc.vector.reciprocal(rden[:, :], den[:, :]).then_inc(fin, 1)
                    nc.vector.tensor_tensor(heads(rcv[:, :]),
                                            heads(XR[:, bass.ds(w, 1), :].rearrange("p o d -> p (o d)")),
                                            wide(has[:, :]), ALU.mult).then_inc(fin, 1)
                elif part == 2:
                    dve.wait_ge(fin, base + 4)
                    nc.vector.tensor_tensor(heads(att[:, :]), heads(ps_sum[0:NW, 0:D]), wide(rden[:, :]), ALU.mult)\
                        .then_inc(fin, 1)

            def moments(w, b, k, part):
                base = w * FIN
                if part == 0:
                    dve.wait_ge(fin, base + 5)
                    nc.vector.tensor_tensor(att2[:, :], att[:, :], rcv[:, :], ALU.subtract).then_inc(fin, 1)
                elif part == 1:
                    dve.wait_ge(x_landed[b], k * 16 + 16)
                    dve.wait_ge(fin, base + 6)
                    nc.vector.tensor_tensor(y[:, :], att2[:, :], x_in[:, b, :], ALU.add).then_inc(fin, 1)
                elif part == 2:
                    dve.wait_ge(fin, base + 7)
                    nc.vector.bn_stats(stats[:, :], y[:, :]).then_inc(fin, 1)
                elif part == 3:
                    wait_apart(dve, fin, base + 8, past_dve)
                    nc.vector.bn_aggr(mv[:, :], stats[:, :]).then_inc(fin, 1)

            def normalise(w, b, k):
                dve.wait_ge(rstd_step, w * 2 + 2)
                dve.wait_ge(stored[b], k * 16 + 1)
                nc.vector.tensor_scalar(y_out[:, b, :], y[:, :], mv[:, 0:1], rstd[:, 0:1], ALU.subtract, ALU.mult)\
                    .then_inc(fin, 1)

            def aside(w, b, k, g, part):
                if g == 3 and there(w - 1):
                    subtract_maxima(w - 1, 1 - b, part)
                if g == 4 and there(w - 2):
                    attended(w - 2, part)
                if g == 5 and there(w - 2):
                    moments(w - 2, b, k - 1, part)
                if g == 6 and there(w + 1) and there(w):
                    prepare(w + 1, 1 - b, k + b if b else k, part)

            def all_messages(w, b, g):
                for m in MSG_NEXT.get(g, []) if there(w - 1) else []:
                    messages(w - 1, 1 - b, m)
                for m in MSG_LAST.get(g, []) if there(w - 2) else []:
                    messages(w - 2, b, m)

            def window(w, b, k):
                for g in range(NG):
                    w1, b1, g1 = after(w, b, g)
                    w0, b0, g0 = before(w, b, g)
                    if there(w1) and there(w):
                        one_hots(w1, b1, g1)
                    if there(w):
                        add_gathered(w, b, k, g)
                    all_messages(w, b, g)
                    if there(w):
                        clamp(w, b, g)
                    aside(w, b, k, g, 0)
                    if there(w0):
                        mish(w0, b0, g0)
                    aside(w, b, k, g, 1)
                    if there(w0):
                        score(w0, b0, g0)
                    aside(w, b, k, g, 2)
                    if there(w0):
                        reduce_heads(w0, b0, g0)
                    aside(w, b, k, g, 3)
                    if g == 0 and there(w - 1):
                        read_heads(w - 1, 1 - b)
                        maxima_in_partitions(w - 1, 1 - b)
                    if g == 2 and there(w - 1):
                        maxima_over_partitions(w - 1)
                    if g == 8 and there(w - 2):
                        normalise(w - 2, b, k - 1)

            for part in range(3):
                prepare(0, 0, 0, part)
            dve.wait_ge(s_table, 16 * 2 * XPARTS)
            one_hots(0, 0, 0)
            run(dve, window)
            general(dve, general_dve)


_INS = ["x", "src", "dst", "edge_attr_128", "L0_gnn_Ws_k", "L0_gnn_Ws_b", "L0_gnn_Wr_k", "L0_gnn_Wr_b",
        "L0_gnn_We_k", "L0_gnn_We_b", "L0_gnn_attn_w", "L0_gnn_attn_b"]


def kernel(**inputs):
    import numpy as _np
    import concourse.bacc as _bacc
    from concourse import mybir as _mybir
    from concourse.bass_utils import run_bass_kernel_spmd as _run

    nc = _bacc.Bacc("TRN2", target_bir_lowering=False, num_devices=1)
    arrays, args = {}, []
    for name in _INS:
        a = _np.ascontiguousarray(inputs[name])
        arrays[f"in_{name}_dram"] = a
        args.append(nc.dram_tensor(f"in_{name}_dram", a.shape, _mybir.dt.from_np(a.dtype), kind="ExternalInput").ap())
    shape = tuple(inputs["x"].shape)
    args.append(nc.dram_tensor("out_0_dram", shape, _mybir.dt.float32, kind="ExternalOutput").ap())
    gat_kernel(nc, *args)
    r = _run(nc, [arrays], core_ids=[0])
    return r.results[0]["out_0_dram"]
```
